# Optimizing a Trainium2 kernel written in Bass

```python
import numpy as np
import jax
import jax.numpy as jnp

def _softmax(x, axis=-1):
    return jax.nn.softmax(x, axis=axis)

def _gelu(x):
    return jax.nn.gelu(x, approximate=True)

def _silu(x):
    return jax.nn.silu(x)

def _sigmoid(x):
    return jax.nn.sigmoid(x)

def _layernorm(x, axis=-1, eps=1e-05):
    m = jnp.mean(x, axis=axis, keepdims=True)
    v = jnp.var(x, axis=axis, keepdims=True)
    return (x - m) / jnp.sqrt(v + eps)

def _scatter_add(tgt, idx, src, axis=0):
    return tgt.at[idx].add(src)

def _segment_sum(src, seg, n):
    return jax.ops.segment_sum(src, seg, n)
kernel_name = 'mk_macaron_d1_jaxref_r8_08d3c1'

def setup_inputs(seed: int=0):
    np.random.seed(seed)
    _w = jnp.asarray

    def _L0_attn_setup():
        import jax, jax.numpy as jnp
        import numpy as np
        LN_EPS = 1e-05
        DENOM_EPS = 1e-06
        NUM_HEADS = 16

        def _layer_norm(x, gamma, beta):
            mu = jnp.mean(x, axis=-1, keepdims=True)
            var = jnp.mean(jnp.square(x - mu), axis=-1, keepdims=True)
            return (x - mu) * jax.lax.rsqrt(var + LN_EPS) * gamma + beta
        key = jax.random.key(seed)
        k1, k2, k3 = jax.random.split(key, 3)
        B, L, D = (4, 512, 128)
        x = jax.random.normal(k1, (B, L, D), dtype=jnp.float32)
        gamma = jnp.ones((D,), dtype=jnp.float32)
        beta = jnp.zeros((D,), dtype=jnp.float32)
        Wqkv = jax.random.normal(k2, (D, 3 * D), dtype=jnp.float32) / np.sqrt(D)
        Wout = jax.random.normal(k3, (D, D), dtype=jnp.float32) / np.sqrt(D)
        return {'x': x, 'gamma': gamma, 'beta': beta, 'Wqkv': Wqkv, 'Wout': Wout}
    _L0_attn_in = _L0_attn_setup()

    def _L0_ffn_setup():
        import jax, jax.numpy as jnp
        import numpy as np
        B, T, C = (4, 256, 128)
        E, H, K = (8, 256, 2)
        key = jax.random.key(seed)
        ks = jax.random.split(key, 7)
        s_in = 1.0 / np.sqrt(C)
        s_hid = 1.0 / np.sqrt(H)
        return {'x': jax.random.normal(ks[0], (B, T, C), dtype=jnp.float32), 'gate_w': jax.random.uniform(ks[1], (C, E), jnp.float32, -s_in, s_in), 'gate_b': jnp.zeros((E,), jnp.float32), 'w1': jax.random.uniform(ks[2], (E, C, H), jnp.float32, -s_in, s_in), 'b1': jax.random.uniform(ks[3], (E, H), jnp.float32, -s_in, s_in), 'w2': jax.random.uniform(ks[4], (E, H, C), jnp.float32, -s_hid, s_hid), 'b2': jax.random.uniform(ks[5], (E, C), jnp.float32, -s_hid, s_hid)}
    _L0_ffn_in = _L0_ffn_setup()
    _d = {'L0_attn_x': _L0_attn_in['x'], 'L0_attn_gamma': _L0_attn_in['gamma'], 'L0_attn_beta': _L0_attn_in['beta'], 'L0_attn_Wqkv': _L0_attn_in['Wqkv'], 'L0_attn_Wout': _L0_attn_in['Wout'], 'L0_ffn_gate_w': _L0_ffn_in['gate_w'], 'L0_ffn_gate_b': _L0_ffn_in['gate_b'], 'L0_ffn_w1': _L0_ffn_in['w1'], 'L0_ffn_b1': _L0_ffn_in['b1'], 'L0_ffn_w2': _L0_ffn_in['w2'], 'L0_ffn_b2': _L0_ffn_in['b2']}
    _x0 = _d['L0_attn_x']
    _d['L0_attn_x'] = jax.random.normal(jax.random.fold_in(jax.random.key(seed), 1), (2, 2048, 128), dtype=_x0.dtype)
    del _x0
    return _d

def reference(L0_attn_x, L0_attn_gamma, L0_attn_beta, L0_attn_Wqkv, L0_attn_Wout, L0_ffn_gate_w, L0_ffn_gate_b, L0_ffn_w1, L0_ffn_b1, L0_ffn_w2, L0_ffn_b2):

    def _L0_attn_ref(x, gamma, beta, Wqkv, Wout):
        import jax, jax.numpy as jnp
        import numpy as np
        LN_EPS = 1e-05
        DENOM_EPS = 1e-06
        NUM_HEADS = 16

        def _layer_norm(x, gamma, beta):
            mu = jnp.mean(x, axis=-1, keepdims=True)
            var = jnp.mean(jnp.square(x - mu), axis=-1, keepdims=True)
            return (x - mu) * jax.lax.rsqrt(var + LN_EPS) * gamma + beta
        B, L, D = x.shape
        H = NUM_HEADS
        HD = D // H
        residual = x
        xn = _layer_norm(x, gamma, beta)
        qkv = (xn @ Wqkv).reshape(B, L, 3, H, HD)
        qkv = jnp.transpose(qkv, (2, 0, 3, 1, 4))
        q, k, v = (qkv[0], qkv[1], qkv[2])
        q = jax.nn.elu(q) + 1.0
        k = jax.nn.elu(k) + 1.0
        kv = jnp.einsum('bhld,bhle->bhde', k, v)
        qkv_out = jnp.einsum('bhld,bhde->bhle', q, kv)
        denom = jnp.einsum('bhld,bhd->bhl', q, k.sum(axis=2)) + DENOM_EPS
        out = qkv_out / denom[..., None]
        out = jnp.transpose(out, (0, 2, 1, 3)).reshape(B, L, D)
        return residual + out @ Wout

    def _L0_ffn_ref(x, gate_w, gate_b, w1, b1, w2, b2):
        import jax, jax.numpy as jnp
        import numpy as np
        B, T, C = (4, 256, 128)
        E, H, K = (8, 256, 2)
        b, t, c = x.shape
        xf = x.reshape(b * t, c)
        logits = xf @ gate_w + gate_b
        probs = jax.nn.softmax(logits, axis=-1)
        gates, expert_idx = jax.lax.top_k(probs, K)
        h = jax.nn.relu(jnp.einsum('nc,ech->neh', xf, w1) + b1)
        expert_out = jnp.einsum('neh,ehc->nec', h, w2) + b2
        onehot = jax.nn.one_hot(expert_idx, E, dtype=xf.dtype)
        weights = jnp.einsum('nk,nke->ne', gates, onehot)
        out = jnp.einsum('ne,nec->nc', weights, expert_out)
        return out.reshape(b, t, c)
    x = L0_attn_x
    x = x + 0.5 * _L0_ffn_ref(_layernorm(x, axis=-1), L0_ffn_gate_w, L0_ffn_gate_b, L0_ffn_w1, L0_ffn_b1, L0_ffn_w2, L0_ffn_b2)
    x = x + _L0_attn_ref(_layernorm(x, axis=-1), L0_attn_gamma, L0_attn_beta, L0_attn_Wqkv, L0_attn_Wout)
    x = x + 0.5 * _L0_ffn_ref(_layernorm(x, axis=-1), L0_ffn_gate_w, L0_ffn_gate_b, L0_ffn_w1, L0_ffn_b1, L0_ffn_w2, L0_ffn_b2)
    return x

_drawn_inputs = setup_inputs


def setup_inputs(seed=0):
    import zlib

    import numpy as np

    out = dict(_drawn_inputs(seed))
    spreads = {'L0_attn_gamma': (1.0, 0.6), 'L0_attn_beta': (0.0, 0.1), 'L0_ffn_gate_b': (0.0, 0.396)}
    factors = {'L0_ffn_b1': 8.0, 'L0_ffn_b2': 6.302}
    for name, (base, spread) in spreads.items():
        noise = np.random.default_rng([zlib.crc32(name.encode()), seed]).standard_normal(out[name].shape)
        drawn = base * np.exp(spread * noise) if base else spread * noise
        out[name] = jnp.asarray(drawn.astype(out[name].dtype))
    for name, factor in factors.items():
        out[name] = (out[name] * factor).astype(out[name].dtype)
    return out
```

```python
from contextlib import ExitStack

import concourse.bass as bass
from concourse import mybir

F32 = mybir.dt.float32
F16 = mybir.dt.float16
ALU = mybir.AluOpType
ACT = mybir.ActivationFunctionType
AX = mybir.AxisListType

P = 128
C = 128
T = 4
NB = T * P
E = 8
J = 2
CH = E * J
NH = 16
HD = C // NH
LAG = 3
ZB = 4
RING = 4
LN_EPS = 1e-5
DENOM_EPS = 1e-6
POOL_LO = (0, 1, 2, 3, 6, 7)
DVE_LO = (4, 5)
STAT_LINKS = 2
TOP_LINKS = 11
LN2_LINKS = 5


def macaron_block(nc, x_in, gamma, beta, w_qkv, w_out, gate_w, gate_b, w1, b1, w2, b2, out):
    batches, seq, _ = x_in.shape
    NBLK = batches * seq // NB
    NS = 2 * NBLK
    BPB = NBLK // batches
    assert (NBLK, BPB, batches) == (8, 4, 2) and w1.shape == (E, C, J * P)
    x_dram = x_in.rearrange("b (n p t) c -> (b n) p (t c)", p=P, t=T)
    out_dram = out.rearrange("b (n p t) c -> (b n) p (t c)", p=P, t=T)

    with ExitStack() as ctx:
        def sb(name, shape, dt=F32):
            return ctx.enter_context(nc.sbuf_tensor(name, shape, dt))

        def bank(name):
            return ctx.enter_context(nc.psum_tensor(name, [P, 512], F32))

        def sem(name):
            return ctx.enter_context(nc.semaphore(name))

        z = [bank(f"z{i}") for i in range(ZB)]
        wb = bank("wb")
        acc = bank("acc")
        tr = bank("tr")
        mi = bank("mi")

        xres = sb("xres", [P, NBLK * T * C])
        w1f = sb("w1f", [P, E, J * P])
        w1h = sb("w1h", [P, E, J * P], F16)
        w1l = sb("w1l", [P, E, J * P], F16)
        w2f = sb("w2f", [P, CH, C])
        w2h = sb("w2h", [P, CH, C], F16)
        w2l = sb("w2l", [P, CH, C], F16)
        gwf = sb("gwf", [P, E])
        gwh = sb("gwh", [P, E], F16)
        gwl = sb("gwl", [P, E], F16)
        gb = sb("gb", [P, E])
        wqkv = sb("wqkv", [P, 3 * C])
        wout = sb("wout", [P, C])
        gam = sb("gam", [P, 1])
        bet = sb("bet", [P, 1])
        b1r = sb("b1r", [CH, P])
        nb1 = sb("nb1", [P, CH])
        b1t = sb("b1t", [P, CH])
        b1m = sb("b1m", [P, CH, 2 * E])
        b2r = sb("b2r", [E, C])
        b2h = sb("b2h", [2 * E, C], F16)
        b2l = sb("b2l", [2 * E, C], F16)
        ident = sb("ident", [P, P])
        ident16 = sb("ident16", [P, P], F16)
        sel = sb("sel", [2 * E, E, P], F16)
        tri = sb("tri", [P, E, E])
        hmask = sb("hmask", [P, NH, HD])
        dmask = sb("dmask", [P, NH])
        cmask = sb("cmask", [P, CH, 2 * E])
        idup = sb("idup", [E, 2 * E])
        nhalf = sb("nhalf", [P, T])
        epst = sb("epst", [P, T])
        st = sb("st", [P, T, 6])
        mv = sb("mv", [P, T, 2])
        ve = sb("ve", [P, T])
        nm = sb("nm", [P, T])
        rs = sb("rs", [P, T])
        xn = sb("xn", [P, T, C])
        xTh = [sb(f"xTh{i}", [P, NB], F16) for i in range(2)]
        xTl = [sb(f"xTl{i}", [P, NB], F16) for i in range(2)]
        lg = sb("lg", [P, T, E])
        mx = sb("mx", [P, T])
        ex = sb("ex", [P, T, E])
        sm = sb("sm", [P, T])
        rsm = sb("rsm", [P, T])
        pr = sb("pr", [P, T, E])
        gt = sb("gt", [P, T, E, E])
        eq = sb("eq", [P, T, E, E])
        rank = sb("rank", [P, T, E])
        gate = sb("gate", [P, T, E])
        g16 = sb("g16", [P, T, 2 * E], F16)
        gT = [sb(f"gT{i}", [2 * E, NB], F16) for i in range(2)]
        wbc = [sb(f"wbc{i}", [P, NB]) for i in range(2)]
        h32 = [sb(f"h32_{i}", [P, J * NB]) for i in range(RING)]
        hhi = [sb(f"hhi{i}", [P, J * NB], F16) for i in range(RING)]
        hlo = [sb(f"hlo{i}", [P, J * NB], F16) for i in range(RING)]
        oT = sb("oT", [P, NB])
        st2 = sb("st2", [P, T, 6])
        mv2 = sb("mv2", [P, T, 2])
        ve2 = sb("ve2", [P, T])
        nm2 = sb("nm2", [P, T])
        r1 = sb("r1", [P, T])
        r1s = sb("r1s", [P, T])
        vy = sb("vy", [P, T])
        vye = sb("vye", [P, T])
        r2 = sb("r2", [P, T])
        r12 = sb("r12", [P, T])
        xs = sb("xs", [P, T, C])
        yn = sb("yn", [P, T, C])
        xn2 = sb("xn2", [P, T, C])
        xn2T = sb("xn2T", [P, NB])
        negq = sb("negq", [P, NB])
        expq = sb("expq", [P, NB])
        negk = sb("negk", [P, NB])
        expk = sb("expk", [P, NB])
        kph = sb("kph", [P, T, C])
        vone = sb("vone", [P, T, C + 1])
        qall = sb("qall", [P, NBLK * NB])
        qcur = sb("qcur", [P, NB])
        kvacc = [sb(f"kvacc{i}", [P, C + 1]) for i in range(batches)]
        kvm = [sb(f"kvm{i}", [P, NH, HD]) for i in range(batches)]
        dm = [sb(f"dm{i}", [P, NH]) for i in range(batches)]
        dene = sb("dene", [P, T, NH])
        rden = sb("rden", [P, T, NH])
        att = sb("att", [P, T, C])
        attT = sb("attT", [P, NB])

        def xblk(b):
            return xres[:, bass.ds(b * (T * C), T * C)]

        def xtile(b, t):
            return xres[:, bass.ds(b * (T * C) + t * C, C)]

        x_here = [sem(f"x_here{i}") for i in range(NBLK)]
        gw_here, gb_here, b1_here, w1_here = sem("gw_here"), sem("gb_here"), sem("b1_here"), sem("w1_here")
        w2_here, b2_here, qkv_here, wo_here = sem("w2_here"), sem("b2_here"), sem("qkv_here"), sem("wo_here")
        gam_here, bet_here = sem("gam_here"), sem("bet_here")
        cst = sem("cst")
        id16_ready = sem("id16_ready")
        gw_split, w1_split, w2_split = sem("gw_split"), sem("w1_split"), sem("w2_split")
        w2h_ready, gwh_ready, w1h_ready = sem("w2h_ready"), sem("gwh_ready"), sem("w1h_ready")
        b1T_ps, b1_ready, nb1_ready = sem("b1T_ps"), sem("b1_ready"), sem("nb1_ready")
        b2_ps, b2h_ready, b2_ready = sem("b2_ps"), sem("b2h_ready"), sem("b2_ready")
        kv_zero = sem("kv_zero")
        wb_ps, wbc_ready = sem("wb_ps"), sem("wbc_ready")
        z_ps, h_ready, hi_ready = sem("z_ps"), sem("h_ready"), sem("hi_ready")
        lo_pool, lo_dve, down_done = sem("lo_pool"), sem("lo_dve"), sem("down_done")
        stat_step, stat_ready, rs_ready, xn_ready = sem("stat_step"), sem("stat_ready"), sem("rs_ready"), sem("xn_ready")
        xT_ps, xTh_ready, xTl_ready = sem("xT_ps"), sem("xTh_ready"), sem("xTl_ready")
        logit_ps, logit_ready, exp_ready = sem("logit_ps"), sem("logit_ready"), sem("exp_ready")
        top_step, gate_ready, gT_ps, gT_ready = sem("top_step"), sem("gate_ready"), sem("gT_ps"), sem("gT_ready")
        oT_ready, o_ps, x_added = sem("oT_ready"), sem("o_ps"), sem("x_added")
        stored = sem("stored")
        stat2_step, stat2_ready, ln2_step = sem("stat2_step"), sem("stat2_ready"), sem("ln2_step")
        xn2_ready, y_ready, y_added = sem("xn2_ready"), sem("y_ready"), sem("y_added")
        r12_ready = sem("r12_ready")
        xn2T_ps, xn2T_ready = sem("xn2T_ps"), sem("xn2T_ready")
        q_ps, q_neg, q_exp, q_ready = sem("q_ps"), sem("q_neg"), sem("q_exp"), sem("q_ready")
        k_ps, k_neg, k_exp, k_ready = sem("k_ps"), sem("k_neg"), sem("k_exp"), sem("k_ready")
        v_ps, v_ready, kv_ps, kv_added = sem("v_ps"), sem("v_ready"), sem("kv_ps"), sem("kv_added")
        kvm_ready = sem("kvm_ready")
        qcur_ready, den_ps, dene_ready, rden_ready = sem("qcur_ready"), sem("den_ps"), sem("dene_ready"), sem("rden_ready")
        num_ps, att_ready, attT_ps, attT_ready = sem("num_ps"), sem("att_ready"), sem("attT_ps"), sem("attT_ready")
        proj_ps, x2_added = sem("proj_ps"), sem("x2_added")

        def has_post(n):
            return n >= 1

        def has_ln2(n):
            return 1 <= n <= NBLK

        def has_kv(n):
            return 2 <= n <= NBLK + 1

        def has_att(n):
            return NBLK - 2 <= n <= NS - 3

        def has_pre(n):
            return n <= NS - 2

        LOOPS = {2: 6, NBLK + 2: NS - 2}

        def run_slots(eng, slot):
            n = 0
            while n < NS:
                if n in LOOPS:
                    with eng.Fori(0, (LOOPS[n] - n) // 2) as i:
                        slot(i * 2 + n, n)
                        slot(i * 2 + (n + 1), n + 1)
                    n = LOOPS[n]
                else:
                    slot(n, n)
                    n += 1

        def chain(eng, s, base, links):
            count = [0]

            def link(ins):
                count[0] += 1
                assert count[0] <= links
                ins.then_inc(s, 1)
                eng.wait_ge(s, base + count[0])
            return link

        block = ctx.enter_context(nc.Block())

        @block.sync
        def _(sp):
            sp.dma_start(xblk(0), x_dram[0]).then_inc(x_here[0], 16)
            sp.dma_start(w1f[:], w1.rearrange("e c h -> c e h")).then_inc(w1_here, 16)
            sp.dma_start(w2f[:], w2.rearrange("e (j p) c -> p (e j) c", p=P)).then_inc(w2_here, 16)
            for b in range(1, NBLK):
                sp.dma_start(xblk(b), x_dram[b]).then_inc(x_here[b], 16)
            for b in range(NBLK):
                sp.wait_ge(x_added, NBLK + b + 1)
                sp.dma_start(out_dram[b], xblk(b)).then_inc(stored, 16)
            sp.wait_ge(stored, 16 * NBLK)

        @block.gpsimd
        def _(pool):
            g = nc.gpsimd
            g.memset(ident[:], 0.0).then_inc(cst, 1)
            g.memset(sel[:], 0.0).then_inc(cst, 1)
            g.memset(tri[:], 1.0).then_inc(cst, 1)
            g.memset(cmask[:], 0.0).then_inc(cst, 1)
            g.memset(idup[:], 0.0).then_inc(cst, 1)
            g.memset(hmask[:], 1.0).then_inc(cst, 1)
            g.memset(dmask[:], 1.0).then_inc(cst, 1)
            g.memset(nhalf[:], -0.5)
            g.memset(epst[:], LN_EPS).then_inc(cst, 1)
            g.memset(vone[:], 1.0).then_inc(cst, 1)
            pool.wait_ge(cst, 9)
            g.affine_select(out=ident[:], in_=ident[:], compare_op=ALU.not_equal, fill=1.0, base=0,
                            pattern=[[-1, P]], channel_multiplier=1).then_inc(cst, 1)
            g.affine_select(out=tri[:], in_=tri[:], compare_op=ALU.is_ge, fill=0.0, base=-1,
                            pattern=[[1, E], [-1, E]], channel_multiplier=0).then_inc(cst, 1)
            g.affine_select(out=sel[:], in_=sel[:], compare_op=ALU.not_equal, fill=1.0, base=0,
                            pattern=[[-1, E], [0, P]], channel_multiplier=1).then_inc(cst, 1)
            g.affine_select(out=cmask[:], in_=cmask[:], compare_op=ALU.not_equal, fill=1.0, base=0,
                            pattern=[[1, E], [0, J], [-1, 2 * E]], channel_multiplier=0).then_inc(cst, 1)
            g.affine_select(out=idup[:], in_=idup[:], compare_op=ALU.not_equal, fill=1.0, base=0,
                            pattern=[[-1, 2 * E]], channel_multiplier=1).then_inc(cst, 1)
            g.affine_select(out=hmask[:], in_=hmask[:], compare_op=ALU.is_ge, fill=0.0, base=0,
                            pattern=[[-HD, NH], [0, HD]], channel_multiplier=1).then_inc(cst, 1)
            g.affine_select(out=dmask[:], in_=dmask[:], compare_op=ALU.is_ge, fill=0.0, base=0,
                            pattern=[[-HD, NH]], channel_multiplier=1).then_inc(cst, 1)
            pool.wait_ge(cst, 16)
            g.affine_select(out=sel[:], in_=sel[:], compare_op=ALU.not_equal, fill=1.0, base=-E,
                            pattern=[[-1, E], [0, P]], channel_multiplier=1).then_inc(cst, 1)

            def rest_of_constants():
                g.affine_select(out=cmask[:], in_=cmask[:], compare_op=ALU.not_equal, fill=1.0, base=E,
                                pattern=[[1, E], [0, J], [-1, 2 * E]], channel_multiplier=0).then_inc(cst, 1)
                g.affine_select(out=idup[:], in_=idup[:], compare_op=ALU.not_equal, fill=1.0, base=E,
                                pattern=[[-1, 2 * E]], channel_multiplier=1).then_inc(cst, 1)
                g.affine_select(out=hmask[:], in_=hmask[:], compare_op=ALU.is_ge, fill=0.0, base=HD - 1,
                                pattern=[[HD, NH], [0, HD]], channel_multiplier=-1).then_inc(cst, 1)
                g.affine_select(out=dmask[:], in_=dmask[:], compare_op=ALU.is_ge, fill=0.0, base=HD - 1,
                                pattern=[[HD, NH]], channel_multiplier=-1).then_inc(cst, 1)

            def root(m):
                pool.wait_ge(stat_ready, m + 1)
                g.tensor_tensor(rs[:], ve[:], nhalf[:], ALU.pow).then_inc(rs_ready, 1)

            def low(n, e):
                pool.wait_ge(hi_ready, n * E + e + 1)
                g.tensor_tensor(hlo[e % RING][:], h32[e % RING][:], hhi[e % RING][:],
                                ALU.subtract).then_inc(lo_pool, 1)

            def second_norm(b):
                link = chain(pool, ln2_step, b * LN2_LINKS, LN2_LINKS)
                pool.wait_ge(stat2_ready, b + 1)
                link(g.tensor_tensor(r1[:], ve2[:], nhalf[:], ALU.pow))
                link(g.tensor_tensor(r1s[:], r1[:], r1[:], ALU.mult))
                link(g.tensor_tensor(vy[:], r1s[:], mv2[:, :, 1], ALU.mult))
                link(g.tensor_tensor(vye[:], vy[:], epst[:], ALU.add))
                link(g.tensor_tensor(r2[:], vye[:], nhalf[:], ALU.pow))
                g.tensor_tensor(r12[:], r1[:], r2[:], ALU.mult).then_inc(r12_ready, 1)

            def add_y(b):
                g.tensor_tensor(xblk(b), xs[:].rearrange("p t c -> p (t c)"),
                                yn[:].rearrange("p t c -> p (t c)"), ALU.add).then_inc(y_added, 1)

            root(0)
            rest_of_constants()

            def slot(n, kind):
                if has_pre(kind):
                    root(n + 1)
                for e in POOL_LO[:4]:
                    low(n, e)
                if has_ln2(kind):
                    second_norm(n - 1)
                for e in POOL_LO[4:-1]:
                    low(n, e)
                if has_ln2(kind):
                    pool.wait_ge(y_ready, n)
                low(n, POOL_LO[-1])
                if has_ln2(kind):
                    add_y(n - 1)

            run_slots(pool, slot)

        @block.scalar
        def _(act):
            a = nc.scalar
            act.dma_start(gwf[:], gate_w).then_inc(gw_here, 16)
            act.dma_start(b1r[:], b1.rearrange("e (j p) -> (e j) p", p=P)).then_inc(b1_here, 16)
            act.dma_start(gb[:], gate_b.partition_broadcast(P)).then_inc(gb_here, 16)
            act.dma_start(b2r[:], b2).then_inc(b2_here, 16)
            act.dma_start(wqkv[:], w_qkv).then_inc(qkv_here, 16)
            act.dma_start(gam[:], gamma.rearrange("(c a) -> c a", a=1)).then_inc(gam_here, 16)
            act.dma_start(bet[:], beta.rearrange("(c a) -> c a", a=1)).then_inc(bet_here, 16)
            act.dma_start(wout[:], w_out).then_inc(wo_here, 16)

            def spread_gates(s):
                act.wait_ge(wb_ps, s + 1)
                a.activation(wbc[0 if spread_gates.even else 1][:], wb[:], ACT.Copy).then_inc(wbc_ready, 1)

            def high(n, e):
                act.wait_ge(h_ready, n * CH + J * e + J)
                a.activation(hhi[e % RING][:], h32[e % RING][:], ACT.Copy).then_inc(hi_ready, 1)

            def x_high(m, par):
                act.wait_ge(xT_ps, m + 1)
                a.activation(xTh[par][:], tr[:], ACT.Copy).then_inc(xTh_ready, 1)

            def gate_exp(m):
                act.wait_ge(logit_ready, m + 1)
                a.activation(ex[:], lg[:], ACT.Exp).then_inc(exp_ready, 1)

            def gates_T(m, par):
                act.wait_ge(gT_ps, m + 1)
                a.activation(gT[par][:], mi[0:2 * E, 0:NB // 2].bitcast(F16), ACT.Copy).then_inc(gT_ready, 1)

            def out_T(m):
                act.wait_ge(down_done, m * E + E)
                if not (isinstance(m, int) and m == 0):
                    act.wait_ge(o_ps, m)
                a.activation(oT[:], acc[:], ACT.Copy, scale=0.5).then_inc(oT_ready, 1)

            def spread(n, e):
                spread_gates.even = e % 2 == 0
                spread_gates(n * E + e)

            x_high(0, 0)
            gate_exp(0)
            gates_T(0, 0)
            act.wait_ge(w2_here, 16)
            a.activation(w2h[:], w2f[:], ACT.Copy).then_inc(w2h_ready, 1)
            spread(0, 0)

            def slot(n, kind):
                par = kind % 2
                for e in range(E):
                    if e == LAG and has_post(kind):
                        out_T(n - 1)
                    if e < E - 1:
                        spread(n, e + 1)
                    elif has_pre(kind):
                        spread(n + 1, 0)
                    high(n, e)
                    if e == 0 and has_att(kind):
                        if kind > NBLK - 2:
                            act.wait_ge(num_ps, n + 2 - NBLK)
                        act.wait_ge(q_ready, n + 2 - NBLK + 1)
                        a.activation(qcur[:], qall[:, bass.ds((n + 2 - NBLK) * NB, NB)],
                                     ACT.Copy).then_inc(qcur_ready, 1)
                    if e == 0 and has_kv(kind):
                        act.wait_ge(k_ps, n - 1)
                        a.activation(negk[:], tr[:], ACT.Relu, scale=-1.0).then_inc(k_neg, 1)
                        act.wait_ge(k_neg, n - 1)
                        a.activation(expk[:], negk[:], ACT.Exp, scale=-1.0).then_inc(k_exp, 1)
                    if e == 1 and has_kv(kind):
                        act.wait_ge(v_ps, n - 1)
                        a.activation(vone[:, :, 0:C], mi[:].rearrange("p (t c) -> p t c", t=T),
                                     ACT.Copy).then_inc(v_ready, 1)
                    if e == 2 and has_pre(kind):
                        x_high(n + 1, 1 - par)
                    if e == 3 and has_pre(kind):
                        gate_exp(n + 1)
                    if e == 3 and has_att(kind):
                        act.wait_ge(attT_ps, n + 2 - NBLK + 1)
                        a.activation(attT[:], tr[:], ACT.Copy).then_inc(attT_ready, 1)
                    if e == 6 and has_pre(kind):
                        gates_T(n + 1, 1 - par)
                    if e == 6 and has_ln2(kind):
                        if kind == 1:
                            act.wait_ge(gam_here, 16)
                            act.wait_ge(bet_here, 16)
                        act.wait_ge(xn2T_ps, n)
                        a.activation(xn2T[:], tr[:], ACT.Identity, bias=bet[:, 0:1],
                                     scale=gam[:, 0:1]).then_inc(xn2T_ready, 1)
                    if e == 7 and has_ln2(kind):
                        act.wait_ge(q_ps, n)
                        a.activation(negq[:], mi[:], ACT.Relu, scale=-1.0).then_inc(q_neg, 1)
                        act.wait_ge(q_neg, n)
                        a.activation(expq[:], negq[:], ACT.Exp, scale=-1.0).then_inc(q_exp, 1)

            run_slots(act, slot)
            out_T(NS - 1)

        @block.vector
        def _(dve):
            v = nc.vector

            def stats(m, tile, s_step, s_ready, st, mv, ve, nm):
                link = chain(dve, s_step, m * STAT_LINKS, STAT_LINKS)
                for t in range(T):
                    last = v.bn_stats(st[:, t, :], tile(t))
                link(last)
                v.tensor_tensor(nm[:], st[:, :, 1], st[:, :, 4], ALU.add)
                for t in range(T):
                    last = v.bn_aggr(mv[:, t, :], st[:, t, :])
                link(last)
                v.tensor_scalar(ve[:], mv[:, :, 1], LN_EPS, None, ALU.add)
                v.tensor_scalar(nm[:], nm[:], -0.5, None, ALU.mult).then_inc(s_ready, 1)

            def first_norm(m, b):
                dve.wait_ge(stat_ready, m + 1)
                dve.wait_ge(rs_ready, m + 1)
                for t in range(T):
                    last = v.tensor_scalar(xn[:, t, :], xtile(b, t), nm[:, t:t + 1], rs[:, t:t + 1],
                                           ALU.add, ALU.mult)
                last.then_inc(xn_ready, 1)

            def second_norm(b):
                dve.wait_ge(r12_ready, b + 1)
                for t in range(T):
                    last = v.tensor_scalar(xn2[:, t, :], xs[:, t, :], nm2[:, t:t + 1], r12[:, t:t + 1],
                                           ALU.add, ALU.mult)
                last.then_inc(xn2_ready, 1)
                for t in range(T):
                    last = v.tensor_scalar(yn[:, t, :], xs[:, t, :], nm2[:, t:t + 1], r1[:, t:t + 1],
                                           ALU.add, ALU.mult)
                last.then_inc(y_ready, 1)

            def x_low(m, par):
                dve.wait_ge(xTh_ready, m + 1)
                v.tensor_tensor(xTl[par][:], tr[:], xTh[par][:], ALU.subtract).then_inc(xTl_ready, 1)

            def gates_a(m):
                link = chain(dve, top_step, m * TOP_LINKS, TOP_LINKS)
                dve.wait_ge(logit_ps, m + 1)
                link(v.tensor_tensor(lg[:], mi[:, 0:T * E].rearrange("p (t e) -> p t e", t=T),
                                     gb[:].unsqueeze(1).broadcast_to([P, T, E]), ALU.add))
                link(v.tensor_reduce(mx[:], lg[:], AX.X, ALU.max))
                v.tensor_tensor(lg[:], lg[:], mx[:].unsqueeze(2).broadcast_to([P, T, E]),
                                ALU.subtract).then_inc(logit_ready, 1)

            def gates_b(m):
                link = chain(dve, top_step, m * TOP_LINKS + 2, TOP_LINKS - 2)
                dve.wait_ge(exp_ready, m + 1)
                link(v.tensor_reduce(sm[:], ex[:], AX.X, ALU.add))
                link(v.reciprocal(rsm[:], sm[:]))
                link(v.tensor_tensor(pr[:], ex[:], rsm[:].unsqueeze(2).broadcast_to([P, T, E]), ALU.mult))
                other = pr[:].unsqueeze(2).broadcast_to([P, T, E, E])
                own = pr[:].unsqueeze(3).broadcast_to([P, T, E, E])
                v.tensor_tensor(gt[:], other, own, ALU.is_gt)
                link(v.tensor_tensor(eq[:], other, own, ALU.is_equal))
                flat = "p t e j -> p t (e j)"
                link(v.tensor_tensor(eq[:].rearrange(flat), eq[:].rearrange(flat),
                                     tri[:].rearrange("p e j -> p (e j)").unsqueeze(1).broadcast_to([P, T, E * E]),
                                     ALU.mult))
                link(v.tensor_tensor(gt[:], gt[:], eq[:], ALU.add))
                link(v.tensor_reduce(rank[:], gt[:], AX.X, ALU.add))
                link(v.scalar_tensor_tensor(out=gate[:], in0=rank[:], scalar=2.0, in1=pr[:],
                                            op0=ALU.is_lt, op1=ALU.mult))
                link(v.tensor_copy(g16[:, :, 0:E], gate[:]))
                v.tensor_tensor(g16[:, :, E:2 * E], gate[:], g16[:, :, 0:E], ALU.subtract).then_inc(gate_ready, 1)

            def add_out(b, m, first):
                dve.wait_ge(o_ps, m + 1)
                v.tensor_tensor(xs[:].rearrange("p t c -> p (t c)") if first else xblk(b), tr[:], xblk(b),
                                ALU.add).then_inc(x_added, 1)

            def hidden(n, e, j):
                c = J * e + j
                if j == 0:
                    dve.wait_ge(wbc_ready, n * E + e + 1)
                dve.wait_ge(z_ps, n * CH + c + 1)
                v.scalar_tensor_tensor(out=h32[e % RING][:, j * NB:(j + 1) * NB], in0=z[c % ZB][:],
                                       scalar=nb1[:, c:c + 1], in1=wbc[e % 2][:],
                                       op0=ALU.max, op1=ALU.mult).then_inc(h_ready, 1)

            def low(n, e):
                dve.wait_ge(hi_ready, n * E + e + 1)
                v.tensor_tensor(hlo[e % RING][:], h32[e % RING][:], hhi[e % RING][:],
                                ALU.subtract).then_inc(lo_dve, 1)

            dve.wait_ge(x_here[0], 16)
            stats(0, lambda t: xtile(0, t), stat_step, stat_ready, st, mv, ve, nm)
            first_norm(0, 0)
            dve.wait_ge(gw_here, 16)
            v.tensor_copy(gwh[:], gwf[:]).then_inc(gwh_ready, 1)
            dve.wait_ge(gwh_ready, 1)
            v.tensor_tensor(gwl[:], gwf[:], gwh[:], ALU.subtract).then_inc(gw_split, 1)
            dve.wait_ge(cst, 16)
            v.tensor_copy(ident16[:], ident[:]).then_inc(id16_ready, 1)
            for i in range(batches):
                last = v.memset(kvacc[i][:], 0.0)
            last.then_inc(kv_zero, 1)
            x_low(0, 0)
            dve.wait_ge(gb_here, 16)
            gates_a(0)
            gates_b(0)
            dve.wait_ge(b1T_ps, 1)
            v.tensor_copy(b1t[:], tr[:, 0:CH]).then_inc(b1_ready, 1)
            v.tensor_scalar(nb1[:], tr[:, 0:CH], -1.0, None, ALU.mult).then_inc(nb1_ready, 1)
            dve.wait_ge(w1_here, 16)
            v.tensor_copy(w1h[:], w1f[:]).then_inc(w1h_ready, 1)
            dve.wait_ge(w1h_ready, 1)
            v.tensor_tensor(w1l[:], w1f[:], w1h[:], ALU.subtract).then_inc(w1_split, 1)
            dve.wait_ge(w2h_ready, 1)
            v.tensor_tensor(w2l[:], w2f[:], w2h[:], ALU.subtract).then_inc(w2_split, 1)
            dve.wait_ge(b1_ready, 1)
            dve.wait_ge(cst, 21)
            v.tensor_tensor(b1m[:], cmask[:], b1t[:].unsqueeze(2).broadcast_to([P, CH, 2 * E]),
                            ALU.mult).then_inc(b1_ready, 1)
            dve.wait_ge(nb1_ready, 1)

            def finish_kv(b):
                dve.wait_ge(kv_added, BPB * (b + 1))
                v.tensor_tensor(kvm[b][:], kvacc[b][:, 0:C].rearrange("p (h d) -> p h d", h=NH), hmask[:],
                                ALU.mult)
                v.tensor_scalar(dm[b][:], dmask[:], kvacc[b][:, C:C + 1], None, ALU.mult).then_inc(kvm_ready, 1)

            def slot(n, kind):
                par = kind % 2
                for e in range(E):
                    if e == 0 and has_pre(kind) and kind + 1 >= NBLK:
                        dve.wait_ge(x2_added, n + 2 - NBLK)
                    hidden(n, e, 0)
                    hidden(n, e, 1)
                    if e - 1 in DVE_LO:
                        low(n, e - 1)
                    if e == 0 and kind == NBLK - 2:
                        finish_kv(0)
                    if e == 0 and has_pre(kind):
                        if kind == 2:
                            for b in range(kind + 1, NBLK):
                                dve.wait_ge(x_here[b], 16)
                        elif kind < 2:
                            dve.wait_ge(x_here[kind + 1], 16)
                        nb = n + 1 if kind + 1 < NBLK else n + 1 - NBLK
                        stats(n + 1, lambda t: xtile(nb, t), stat_step, stat_ready, st, mv, ve, nm)
                    if e == 0 and has_kv(kind):
                        dve.wait_ge(k_exp, n - 1)
                        v.scalar_tensor_tensor(out=kph[:].rearrange("p t c -> p (t c)"), in0=tr[:], scalar=0.0,
                                               in1=expk[:], op0=ALU.max, op1=ALU.add).then_inc(k_ready, 1)
                    if e == 0 and has_att(kind):
                        dve.wait_ge(den_ps, n + 3 - NBLK)
                        v.tensor_scalar(dene[:], mi[:, 0:T * NH].rearrange("p (t h) -> p t h", t=T), DENOM_EPS,
                                        None, ALU.add).then_inc(dene_ready, 1)
                        dve.wait_ge(dene_ready, n + 3 - NBLK)
                        v.reciprocal(rden[:], dene[:]).then_inc(rden_ready, 1)
                    if e == 0 and has_pre(kind):
                        first_norm(n + 1, nb)
                    if e == 1 and has_att(kind):
                        dve.wait_ge(rden_ready, n + 3 - NBLK)
                        dve.wait_ge(num_ps, n + 3 - NBLK)
                        v.tensor_tensor(att[:].rearrange("p t (h d) -> p (t h) d", h=NH),
                                        tr[:].rearrange("p (g d) -> p g d", d=HD),
                                        rden[:].rearrange("p t h -> p (t h)").unsqueeze(2).broadcast_to([P, T * NH, HD]),
                                        ALU.mult).then_inc(att_ready, 1)
                    if e == 2 and has_kv(kind):
                        acc_b = 0 if kind < 2 + BPB else 1
                        dve.wait_ge(kv_ps, n - 1)
                        if kind == 2:
                            dve.wait_ge(kv_zero, 1)
                        else:
                            dve.wait_ge(kv_added, n - 2)
                        v.tensor_tensor(kvacc[acc_b][:], mi[:, 0:C + 1], kvacc[acc_b][:],
                                        ALU.add).then_inc(kv_added, 1)
                        if kind == NBLK + 1:
                            finish_kv(1)
                    if e == 2 and has_pre(kind):
                        x_low(n + 1, 1 - par)
                    if e == 3 and has_pre(kind):
                        gates_a(n + 1)
                    if e == 4 and has_post(kind):
                        m = n - 1
                        b = m if kind - 1 < NBLK else m - NBLK
                        if has_ln2(kind) and kind > 1:
                            dve.wait_ge(y_added, n - 1)
                        add_out(b, m, has_ln2(kind))
                        if has_ln2(kind):
                            dve.wait_ge(x_added, n)
                            stats(m, lambda t: xs[:, t, :], stat2_step, stat2_ready, st2, mv2, ve2, nm2)
                    if e == 4 and has_pre(kind):
                        gates_b(n + 1)
                    if e == 5 and has_ln2(kind):
                        second_norm(n - 1)
                    if e == 5 and has_att(kind):
                        b = n + 2 - NBLK
                        dve.wait_ge(proj_ps, b + 1)
                        dve.wait_ge(y_added, b + 1)
                        v.tensor_tensor(xblk(b), tr[:], xblk(b), ALU.add).then_inc(x2_added, 1)
                    if kind == 0 and e == 4:
                        dve.wait_ge(b2_ps, 1)
                        v.tensor_copy(b2h[:], tr[0:2 * E, 0:C]).then_inc(b2h_ready, 1)
                        dve.wait_ge(b2h_ready, 1)
                        v.tensor_tensor(b2l[:], tr[0:2 * E, 0:C], b2h[:], ALU.subtract).then_inc(b2_ready, 1)
                    if e == 7 and has_ln2(kind):
                        dve.wait_ge(q_exp, n)
                        v.scalar_tensor_tensor(out=qall[:, bass.ds((n - 1) * NB, NB)], in0=mi[:], scalar=0.0,
                                               in1=expq[:], op0=ALU.max, op1=ALU.add).then_inc(q_ready, 1)

            run_slots(dve, slot)
            add_out(NBLK - 1, NS - 1, False)

        @block.tensor
        def _(pe):
            mm = nc.tensor.matmul

            def spread(n, e, par):
                if not (isinstance(n, int) and n == 0 and e == 0):
                    pe.wait_ge(wbc_ready, n * E + e)
                if e == 0:
                    pe.wait_ge(gT_ready, n + 1)
                mm(wb[:], sel[:, e, :], gT[par][:], start=True, stop=True).then_inc(wb_ps, 1)

            def up(n, kind, e, par):
                for j in range(J):
                    c = J * e + j
                    if kind > 0 or c >= ZB:
                        pe.wait_ge(h_ready, n * CH + c + 1 - ZB)
                    zb = z[c % ZB][:]
                    wh, wl = (w[:, e, j * P:(j + 1) * P] for w in (w1h, w1l))
                    mm(zb, wh, xTh[par][:], start=True, stop=False)
                    mm(zb, wh, xTl[par][:], start=False, stop=False)
                    mm(zb, wl, xTh[par][:], start=False, stop=True).then_inc(z_ps, 1)

            def down(n, e, par):
                if e in POOL_LO:
                    pe.wait_ge(lo_pool, n * len(POOL_LO) + POOL_LO.index(e) + 1)
                else:
                    pe.wait_ge(lo_dve, n * len(DVE_LO) + DVE_LO.index(e) + 1)
                if e == 0 and not (isinstance(n, int) and n == 0):
                    pe.wait_ge(oT_ready, n)
                if e == E - 1:
                    mm(acc[:], b2h[:], gT[par][:], start=False, stop=False)
                    mm(acc[:], b2l[:], gT[par][:], start=False, stop=False)
                for j in range(J):
                    c = J * e + j
                    hh, hl = (h[e % RING][:, j * NB:(j + 1) * NB] for h in (hhi, hlo))
                    mm(acc[:], w2h[:, c, :], hh, start=(c == 0), stop=False)
                    mm(acc[:], w2l[:, c, :], hh, start=False, stop=False)
                    last = mm(acc[:], w2h[:, c, :], hl, start=False, stop=(c == CH - 1))
                last.then_inc(down_done, 1)

            def transposes(dst, src, signal):
                for t in range(T):
                    last = nc.tensor.transpose(dst[:, t * P:(t + 1) * P], src(t), ident[:])
                last.then_inc(signal, 1)

            def logits(m, par):
                pe.wait_ge(xTl_ready, m + 1)
                for t in range(T):
                    xh, xl = (x[par][:, t * P:(t + 1) * P] for x in (xTh, xTl))
                    o = mi[:, t * E:(t + 1) * E]
                    mm(o, xh, gwh[:], start=True, stop=False)
                    mm(o, xh, gwl[:], start=False, stop=False)
                    last = mm(o, xl, gwh[:], start=False, stop=True)
                last.then_inc(logit_ps, 1)

            def gates_T(m):
                pe.wait_ge(gate_ready, m + 1)
                o = mi[0:2 * E, 0:NB // 2].bitcast(F16)
                for t in range(T):
                    last = nc.tensor.transpose(o[:, t * P:(t + 1) * P], g16[:, t, :], ident16[:])
                last.then_inc(gT_ps, 1)

            pe.wait_ge(cst, 16)
            pe.wait_ge(xn_ready, 1)
            transposes(tr, lambda t: xn[:, t, :], xT_ps)
            pe.wait_ge(gw_split, 1)
            logits(0, 0)
            pe.wait_ge(b1_here, 16)
            nc.tensor.transpose(tr[:, 0:CH], b1r[:], ident[0:CH, 0:CH]).then_inc(b1T_ps, 1)
            pe.wait_ge(id16_ready, 1)
            gates_T(0)
            pe.wait_ge(cst, 17)
            spread(0, 0, 0)
            pe.wait_ge(w1_split, 1)

            def side(n, kind, e):
                par = kind % 2
                if e == 0 and has_kv(kind):
                    pe.wait_ge(xn2T_ready, n - 1)
                    for t in range(T):
                        last = mm(tr[:, t * C:(t + 1) * C], xn2T[:, t * P:(t + 1) * P], wqkv[:, C:2 * C],
                                  start=True, stop=True)
                    last.then_inc(k_ps, 1)
                if e == 0 and has_att(kind):
                    m = n + 2 - NBLK
                    b = 0 if kind + 2 - NBLK < BPB else 1
                    if has_kv(kind):
                        pe.wait_ge(q_ready, n - 1)
                    else:
                        pe.wait_ge(gT_ready, n + 1)
                    pe.wait_ge(kvm_ready, b + 1)
                    pe.wait_ge(qcur_ready, m + 1)
                    for t in range(T):
                        last = mm(mi[:, t * NH:(t + 1) * NH], qcur[:, t * P:(t + 1) * P], dm[b][:],
                                  start=True, stop=True)
                    last.then_inc(den_ps, 1)
                if e == 1 and has_att(kind):
                    m = n + 2 - NBLK
                    b = 0 if kind + 2 - NBLK < BPB else 1
                    if has_kv(kind):
                        pe.wait_ge(k_ready, n - 1)
                    else:
                        pe.wait_ge(x2_added, m)
                    for t in range(T):
                        last = mm(tr[:, t * C:(t + 1) * C], qcur[:, t * P:(t + 1) * P],
                                  kvm[b][:].rearrange("p h d -> p (h d)"), start=True, stop=True)
                    last.then_inc(num_ps, 1)
                if e == 1 and has_kv(kind):
                    pe.wait_ge(q_ready, n - 1)
                    if has_att(kind):
                        pe.wait_ge(dene_ready, n + 3 - NBLK)
                    for t in range(T):
                        last = mm(mi[:, t * C:(t + 1) * C], xn2T[:, t * P:(t + 1) * P], wqkv[:, 2 * C:3 * C],
                                  start=True, stop=True)
                    last.then_inc(v_ps, 1)
                if e == 2 and has_kv(kind):
                    pe.wait_ge(k_ready, n - 1)
                    pe.wait_ge(v_ready, n - 1)
                    for t in range(T):
                        last = mm(mi[:, 0:C + 1], kph[:, t, :], vone[:, t, :], start=(t == 0), stop=(t == T - 1))
                    last.then_inc(kv_ps, 1)
                if e == 2 and has_pre(kind):
                    pe.wait_ge(xn_ready, n + 2)
                    if has_att(kind):
                        pe.wait_ge(att_ready, n + 3 - NBLK)
                    elif has_kv(kind):
                        pe.wait_ge(k_ready, n - 1)
                    elif kind > NBLK:
                        pe.wait_ge(x2_added, NBLK)
                    elif kind == 1:
                        pe.wait_ge(b2_ready, 1)
                    else:
                        pe.wait_ge(nb1_ready, 1)
                    transposes(tr, lambda t: xn[:, t, :], xT_ps)
                if e == 3 and has_pre(kind):
                    if has_kv(kind):
                        pe.wait_ge(kv_added, n - 1)
                    elif has_att(kind):
                        pe.wait_ge(dene_ready, n + 3 - NBLK)
                    else:
                        pe.wait_ge(gT_ready, n + 1)
                    logits(n + 1, 1 - par)
                if e == 3 and has_att(kind):
                    pe.wait_ge(att_ready, n + 3 - NBLK)
                    pe.wait_ge(xTl_ready, n + 2)
                    transposes(tr, lambda t: att[:, t, :], attT_ps)
                if e == 4 and has_post(kind):
                    pe.wait_ge(oT_ready, n)
                    if has_att(kind):
                        pe.wait_ge(attT_ready, n + 3 - NBLK)
                    elif has_pre(kind):
                        pe.wait_ge(xTl_ready, n + 2)
                    else:
                        pe.wait_ge(x_added, n - 1)
                    transposes(tr, lambda t: oT[:, t * P:(t + 1) * P], o_ps)
                if e == 4 and kind == 0:
                    pe.wait_ge(b1_ready, 2)
                    pe.wait_ge(b2_here, 16)
                    pe.wait_ge(xTl_ready, 2)
                    o = tr[0:2 * E, 0:C]
                    mm(o, idup[:], b2r[:], start=True, stop=False)
                    for c in range(CH):
                        last = mm(o, b1m[:, c, :], w2f[:, c, :], start=False, stop=(c == CH - 1))
                    last.then_inc(b2_ps, 1)
                if e == 5 and has_att(kind):
                    pe.wait_ge(attT_ready, n + 3 - NBLK)
                    pe.wait_ge(x_added, n)
                    for t in range(T):
                        last = mm(tr[:, t * C:(t + 1) * C], attT[:, t * P:(t + 1) * P], wout[:],
                                  start=True, stop=True)
                    last.then_inc(proj_ps, 1)
                if e == 6 and has_pre(kind):
                    gates_T(n + 1)
                if e == 6 and has_ln2(kind):
                    pe.wait_ge(xn2_ready, n)
                    if has_att(kind):
                        pe.wait_ge(x2_added, n + 3 - NBLK)
                    transposes(tr, lambda t: xn2[:, t, :], xn2T_ps)
                if e == 7 and has_ln2(kind):
                    pe.wait_ge(xn2T_ready, n)
                    pe.wait_ge(gT_ready, n + 2)
                    mm(mi[:], wqkv[:, 0:C], xn2T[:], start=True, stop=True).then_inc(q_ps, 1)

            def slot(n, kind):
                par = kind % 2
                if kind == 1:
                    pe.wait_ge(qkv_here, 16)
                    pe.wait_ge(wo_here, 16)
                    pe.wait_ge(b2_ready, 1)
                for e in range(E):
                    if e < E - 1:
                        spread(n, e + 1, par)
                    elif has_pre(kind):
                        spread(n + 1, 0, 1 - par)
                    up(n, kind, e, par)
                    side(n, kind, e)
                    if kind == 0 and e == LAG:
                        pe.wait_ge(w2_split, 1)
                    if e >= LAG:
                        down(n, e - LAG, par)
                    elif kind > 0:
                        down(n - 1, E + e - LAG, 1 - par)

            run_slots(pe, slot)
            for e in range(E - LAG, E):
                down(NS - 1, e, (NS - 1) % 2)
            pe.wait_ge(oT_ready, NS)
            pe.wait_ge(x_added, NS - 1)
            transposes(tr, lambda t: oT[:, t * P:(t + 1) * P], o_ps)


_INS = ['L0_attn_x', 'L0_attn_gamma', 'L0_attn_beta', 'L0_attn_Wqkv', 'L0_attn_Wout', 'L0_ffn_gate_w',
        'L0_ffn_gate_b', 'L0_ffn_w1', 'L0_ffn_b1', 'L0_ffn_w2', 'L0_ffn_b2']
_OUTS = [((2, 2048, 128), 'float32')]


def kernel(**inputs):
    import numpy as _np
    import concourse.bacc as _bacc
    from concourse import mybir as _mybir
    from concourse.bass_utils import run_bass_kernel_spmd as _run

    nc = _bacc.Bacc("TRN2", target_bir_lowering=False, num_devices=1)
    arrays, args = {}, []
    for name in _INS:
        a = _np.ascontiguousarray(inputs[name])
        arrays[f"in_{name}_dram"] = a
        args.append(nc.dram_tensor(f"in_{name}_dram", a.shape, _mybir.dt.from_np(a.dtype), kind="ExternalInput").ap())
    for i, (shape, dtype) in enumerate(_OUTS):
        dt = _mybir.dt.from_np(_np.dtype(dtype))
        args.append(nc.dram_tensor(f"out_{i}_dram", shape, dt, kind="ExternalOutput").ap())
    macaron_block(nc, *args)
    r = _run(nc, [arrays], core_ids=[0])
    got = tuple(r.results[0][f"out_{i}_dram"] for i in range(len(_OUTS)))
    return got[0]
```

```python
from contextlib import ExitStack

import concourse.bass as bass
from concourse import mybir

F32 = mybir.dt.float32
F16 = mybir.dt.float16
ALU = mybir.AluOpType
ACT = mybir.ActivationFunctionType
AX = mybir.AxisListType

P = 128
C = 128
T = 4
NB = T * P
E = 8
J = 2
CH = E * J
NH = 16
HD = C // NH
LAG = 3
ZB = 4
RING = 4
EARLY = 2
LN_EPS = 1e-5
DENOM_EPS = 1e-6
POOL_LO = (0, 1, 2, 4, 6, 7)
DVE_LO = (3, 5)
STAT_LINKS = 2
TOP_LINKS = 11
LN2_LINKS = 5


def macaron_block(nc, x_in, gamma, beta, w_qkv, w_out, gate_w, gate_b, w1, b1, w2, b2, out):
    batches, seq, _ = x_in.shape
    NBLK = batches * seq // NB
    NS = 2 * NBLK
    BPB = NBLK // batches
    assert (NBLK, BPB, batches) == (8, 4, 2) and w1.shape == (E, C, J * P)
    x_dram = x_in.rearrange("b (n p t) c -> (b n) p (t c)", p=P, t=T)
    out_dram = out.rearrange("b (n p t) c -> (b n) p (t c)", p=P, t=T)

    with ExitStack() as ctx:
        def sb(name, shape, dt=F32):
            return ctx.enter_context(nc.sbuf_tensor(name, shape, dt))

        def bank(name):
            return ctx.enter_context(nc.psum_tensor(name, [P, 512], F32))

        def sem(name):
            return ctx.enter_context(nc.semaphore(name))

        z = [bank(f"z{i}") for i in range(ZB)]
        wb = bank("wb")
        acc = bank("acc")
        tr = bank("tr")
        mi = bank("mi")

        xres = sb("xres", [P, NBLK * T * C])
        w1f = sb("w1f", [P, E, J * P])
        w1h = sb("w1h", [P, E, J * P], F16)
        w1l = sb("w1l", [P, E, J * P], F16)
        w2f = sb("w2f", [P, CH, C])
        w2h = sb("w2h", [P, CH, C], F16)
        w2l = sb("w2l", [P, CH, C], F16)
        gwf = sb("gwf", [P, E])
        gwh = sb("gwh", [P, E], F16)
        gwl = sb("gwl", [P, E], F16)
        gb = sb("gb", [P, E])
        wqkv = sb("wqkv", [P, 3 * C])
        wout = sb("wout", [P, C])
        gam = sb("gam", [P, 1])
        bet = sb("bet", [P, 1])
        b1r = sb("b1r", [CH, P])
        nb1 = sb("nb1", [P, CH])
        b1t = sb("b1t", [P, CH])
        b1m = sb("b1m", [P, CH, 2 * E])
        b2r = sb("b2r", [E, C])
        b2h = sb("b2h", [2 * E, C], F16)
        b2l = sb("b2l", [2 * E, C], F16)
        ident = sb("ident", [P, P])
        ident16 = sb("ident16", [P, P], F16)
        sel = sb("sel", [2 * E, E, P], F16)
        tri = sb("tri", [P, E, E])
        hmask = sb("hmask", [P, NH, HD])
        dmask = sb("dmask", [P, NH])
        cmask = sb("cmask", [P, CH, 2 * E])
        idup = sb("idup", [E, 2 * E])
        nhalf = sb("nhalf", [P, T])
        epst = sb("epst", [P, T])
        st = sb("st", [P, T, 6])
        mv = sb("mv", [P, T, 2])
        ve = sb("ve", [P, T])
        nm = sb("nm", [P, T])
        rs = sb("rs", [P, T])
        xn = sb("xn", [P, T, C])
        xTh = [sb(f"xTh{i}", [P, NB], F16) for i in range(2)]
        xTl = [sb(f"xTl{i}", [P, NB], F16) for i in range(2)]
        lg = sb("lg", [P, T, E])
        mx = sb("mx", [P, T])
        ex = sb("ex", [P, T, E])
        sm = sb("sm", [P, T])
        rsm = sb("rsm", [P, T])
        pr = sb("pr", [P, T, E])
        gt = sb("gt", [P, T, E, E])
        eq = sb("eq", [P, T, E, E])
        rank = sb("rank", [P, T, E])
        gate = sb("gate", [P, T, E])
        g16 = sb("g16", [P, T, 2 * E], F16)
        gT = [sb(f"gT{i}", [2 * E, NB], F16) for i in range(2)]
        wbc = [sb(f"wbc{i}", [P, NB]) for i in range(2)]
        h32 = [sb(f"h32_{i}", [P, J * NB]) for i in range(RING)]
        hhi = [sb(f"hhi{i}", [P, J * NB], F16) for i in range(RING)]
        hlo = [sb(f"hlo{i}", [P, J * NB], F16) for i in range(RING)]
        oT = sb("oT", [P, NB])
        st2 = sb("st2", [P, T, 6])
        mv2 = sb("mv2", [P, T, 2])
        ve2 = sb("ve2", [P, T])
        nm2 = sb("nm2", [P, T])
        r1 = sb("r1", [P, T])
        r1s = sb("r1s", [P, T])
        vy = sb("vy", [P, T])
        vye = sb("vye", [P, T])
        r2 = sb("r2", [P, T])
        r12 = sb("r12", [P, T])
        xs = sb("xs", [P, T, C])
        yc = sb("yc", [P, T, C])
        yn = sb("yn", [P, T, C])
        xn2 = sb("xn2", [P, T, C])
        xn2T = sb("xn2T", [P, NB])
        negq = sb("negq", [P, NB])
        expq = sb("expq", [P, NB])
        negk = sb("negk", [P, NB])
        expk = sb("expk", [P, NB])
        posk = sb("posk", [P, NB])
        posq = sb("posq", [P, NB])
        kph = sb("kph", [P, T, C])
        vone = sb("vone", [P, T, C + 1])
        qall = sb("qall", [P, NBLK * NB])
        qcur = sb("qcur", [P, NB])
        kvacc = [sb(f"kvacc{i}", [P, C + 1]) for i in range(batches)]
        kvm = [sb(f"kvm{i}", [P, NH, HD]) for i in range(batches)]
        dm = [sb(f"dm{i}", [P, NH]) for i in range(batches)]
        dene = sb("dene", [P, T, NH])
        rden = sb("rden", [P, T, NH])
        att = sb("att", [P, T, C])
        attT = sb("attT", [P, NB])

        def xblk(b):
            return xres[:, bass.ds(b * (T * C), T * C)]

        def xtile(b, t):
            return xres[:, bass.ds(b * (T * C) + t * C, C)]

        x_here = [sem(f"x_here{i}") for i in range(NBLK)]
        gw_here, gb_here, b1_here = sem("gw_here"), sem("gb_here"), sem("b1_here")
        w1_here = [sem("w1_here0"), sem("w1_here1")]
        w2_here, b2_here, qkv_here, wo_here = sem("w2_here"), sem("b2_here"), sem("qkv_here"), sem("wo_here")
        gam_here, bet_here = sem("gam_here"), sem("bet_here")
        cst = sem("cst")
        id16_ready = sem("id16_ready")
        gw_split, w1_split, w2_split = sem("gw_split"), sem("w1_split"), sem("w2_split")
        w2h_ready, gwh_ready, w1h_ready = sem("w2h_ready"), sem("gwh_ready"), sem("w1h_ready")
        b1T_ps, b1_ready, nb1_ready = sem("b1T_ps"), sem("b1_ready"), sem("nb1_ready")
        b2_ps, b2h_ready, b2_ready = sem("b2_ps"), sem("b2h_ready"), sem("b2_ready")
        kv_zero = sem("kv_zero")
        wb_ps, wbc_ready = sem("wb_ps"), sem("wbc_ready")
        z_ps, h_ready, hi_ready = sem("z_ps"), sem("h_ready"), sem("hi_ready")
        lo_pool, lo_dve, down_done = sem("lo_pool"), sem("lo_dve"), sem("down_done")
        stat_step, stat_ready, rs_ready, xn_ready = sem("stat_step"), sem("stat_ready"), sem("rs_ready"), sem("xn_ready")
        xT_ps, xTh_ready, xTl_ready = sem("xT_ps"), sem("xTh_ready"), sem("xTl_ready")
        logit_ps, logit_ready, exp_ready = sem("logit_ps"), sem("logit_ready"), sem("exp_ready")
        top_step, gate_ready, gT_ps, gT_ready = sem("top_step"), sem("gate_ready"), sem("gT_ps"), sem("gT_ready")
        oT_ready, o_ps, x_added = sem("oT_ready"), sem("o_ps"), sem("x_added")
        stored = sem("stored")
        stat2_step, stat2_ready, ln2_step = sem("stat2_step"), sem("stat2_ready"), sem("ln2_step")
        xn2_ready, y_step, y_added = sem("xn2_ready"), sem("y_step"), sem("y_added")
        r12_ready = sem("r12_ready")
        xn2T_ps, xn2T_ready = sem("xn2T_ps"), sem("xn2T_ready")
        q_ps, q_neg, q_pos, q_exp, q_ready = sem("q_ps"), sem("q_neg"), sem("q_pos"), sem("q_exp"), sem("q_ready")
        k_ps, k_neg, k_pos, k_exp, k_ready = sem("k_ps"), sem("k_neg"), sem("k_pos"), sem("k_exp"), sem("k_ready")
        v_ps, v_ready, kv_ps, kv_added = sem("v_ps"), sem("v_ready"), sem("kv_ps"), sem("kv_added")
        kvm_ready = sem("kvm_ready")
        qcur_ready, den_ps, dene_ready, rden_ready = sem("qcur_ready"), sem("den_ps"), sem("dene_ready"), sem("rden_ready")
        num_ps, att_ready, attT_ps, attT_ready = sem("num_ps"), sem("att_ready"), sem("attT_ps"), sem("attT_ready")
        proj_ps, x2_added = sem("proj_ps"), sem("x2_added")

        def has_post(n):
            return n >= 1

        def has_ln2(n):
            return 1 <= n <= NBLK

        def has_kv(n):
            return 2 <= n <= NBLK + 1

        def has_att(n):
            return NBLK - 2 <= n <= NS - 3

        def has_pre(n):
            return n <= NS - 2

        LOOPS = {2: 6, NBLK + 2: NS - 2}

        def run_slots(eng, slot):
            n = 0
            while n < NS:
                if n in LOOPS:
                    with eng.Fori(0, (LOOPS[n] - n) // 2) as i:
                        slot(i * 2 + n, n)
                        slot(i * 2 + (n + 1), n + 1)
                    n = LOOPS[n]
                else:
                    slot(n, n)
                    n += 1

        def chain(eng, s, base, links):
            count = [0]

            def link(ins):
                count[0] += 1
                assert count[0] <= links
                ins.then_inc(s, 1)
                eng.wait_ge(s, base + count[0])
            return link

        block = ctx.enter_context(nc.Block())

        @block.sync
        def _(sp):
            sp.dma_start(xblk(0), x_dram[0]).then_inc(x_here[0], 16)
            w1_dram = w1.rearrange("e c h -> c e h")
            sp.dma_start(w1f[:, 0:EARLY], w1_dram[:, 0:EARLY]).then_inc(w1_here[0], 16)
            sp.dma_start(w1f[:, EARLY:E], w1_dram[:, EARLY:E]).then_inc(w1_here[1], 16)
            sp.dma_start(w2f[:], w2.rearrange("e (j p) c -> p (e j) c", p=P)).then_inc(w2_here, 16)
            for b in range(1, NBLK):
                sp.dma_start(xblk(b), x_dram[b]).then_inc(x_here[b], 16)
            for b in range(NBLK):
                sp.wait_ge(x_added, NBLK + b + 1)
                sp.dma_start(out_dram[b], xblk(b)).then_inc(stored, 16)
            sp.wait_ge(stored, 16 * NBLK)

        @block.gpsimd
        def _(pool):
            g = nc.gpsimd
            g.memset(nhalf[:], -0.5).then_inc(cst, 1)
            g.memset(ident[:], 0.0).then_inc(cst, 1)
            pool.wait_ge(cst, 2)
            g.affine_select(out=ident[:], in_=ident[:], compare_op=ALU.not_equal, fill=1.0, base=0,
                            pattern=[[-1, P]], channel_multiplier=1).then_inc(cst, 1)

            def masks():
                g.memset(tri[:], 1.0).then_inc(cst, 1)
                g.memset(sel[:], 0.0).then_inc(cst, 1)
                g.memset(cmask[:], 0.0).then_inc(cst, 1)
                g.memset(idup[:], 0.0).then_inc(cst, 1)
                g.memset(hmask[:], 1.0).then_inc(cst, 1)
                g.memset(dmask[:], 1.0).then_inc(cst, 1)
                g.memset(epst[:], LN_EPS).then_inc(cst, 1)
                g.memset(vone[:], 1.0).then_inc(cst, 1)
                pool.wait_ge(cst, 11)
                g.affine_select(out=tri[:], in_=tri[:], compare_op=ALU.is_ge, fill=0.0, base=-1,
                                pattern=[[1, E], [-1, E]], channel_multiplier=0).then_inc(cst, 1)
                g.affine_select(out=sel[:], in_=sel[:], compare_op=ALU.not_equal, fill=1.0, base=0,
                                pattern=[[-1, E], [0, P]], channel_multiplier=1).then_inc(cst, 1)
                g.affine_select(out=cmask[:], in_=cmask[:], compare_op=ALU.not_equal, fill=1.0, base=0,
                                pattern=[[1, E], [0, J], [-1, 2 * E]], channel_multiplier=0).then_inc(cst, 1)
                g.affine_select(out=idup[:], in_=idup[:], compare_op=ALU.not_equal, fill=1.0, base=0,
                                pattern=[[-1, 2 * E]], channel_multiplier=1).then_inc(cst, 1)
                g.affine_select(out=hmask[:], in_=hmask[:], compare_op=ALU.is_ge, fill=0.0, base=0,
                                pattern=[[-HD, NH], [0, HD]], channel_multiplier=1).then_inc(cst, 1)
                g.affine_select(out=dmask[:], in_=dmask[:], compare_op=ALU.is_ge, fill=0.0, base=0,
                                pattern=[[-HD, NH]], channel_multiplier=1).then_inc(cst, 1)
                pool.wait_ge(cst, 17)
                g.affine_select(out=sel[:], in_=sel[:], compare_op=ALU.not_equal, fill=1.0, base=-E,
                                pattern=[[-1, E], [0, P]], channel_multiplier=1).then_inc(cst, 1)
                g.affine_select(out=cmask[:], in_=cmask[:], compare_op=ALU.not_equal, fill=1.0, base=E,
                                pattern=[[1, E], [0, J], [-1, 2 * E]], channel_multiplier=0).then_inc(cst, 1)
                g.affine_select(out=idup[:], in_=idup[:], compare_op=ALU.not_equal, fill=1.0, base=E,
                                pattern=[[-1, 2 * E]], channel_multiplier=1).then_inc(cst, 1)
                g.affine_select(out=hmask[:], in_=hmask[:], compare_op=ALU.is_ge, fill=0.0, base=HD - 1,
                                pattern=[[HD, NH], [0, HD]], channel_multiplier=-1).then_inc(cst, 1)
                g.affine_select(out=dmask[:], in_=dmask[:], compare_op=ALU.is_ge, fill=0.0, base=HD - 1,
                                pattern=[[HD, NH]], channel_multiplier=-1).then_inc(cst, 1)

            def root(m):
                pool.wait_ge(stat_ready, m + 1)
                g.tensor_tensor(rs[:], ve[:], nhalf[:], ALU.pow).then_inc(rs_ready, 1)

            def low(n, e):
                pool.wait_ge(hi_ready, n * E + e + 1)
                g.tensor_tensor(hlo[e % RING][:], h32[e % RING][:], hhi[e % RING][:],
                                ALU.subtract).then_inc(lo_pool, 1)

            def second_roots(b):
                link = chain(pool, ln2_step, b * LN2_LINKS, LN2_LINKS)
                pool.wait_ge(stat2_ready, b + 1)
                link(g.tensor_tensor(r1[:], ve2[:], nhalf[:], ALU.pow))
                link(g.tensor_tensor(r1s[:], r1[:], r1[:], ALU.mult))
                link(g.tensor_tensor(vy[:], r1s[:], mv2[:, :, 1], ALU.mult))
                link(g.tensor_tensor(vye[:], vy[:], epst[:], ALU.add))
                link(g.tensor_tensor(r2[:], vye[:], nhalf[:], ALU.pow))
                g.tensor_tensor(r12[:], r1[:], r2[:], ALU.mult).then_inc(r12_ready, 1)

            def y_of(b):
                g.tensor_tensor(yc[:], xs[:], nm2[:].unsqueeze(2).broadcast_to([P, T, C]), ALU.add).then_inc(y_step, 1)
                pool.wait_ge(y_step, 2 * b + 1)
                g.tensor_tensor(yn[:], yc[:], r1[:].unsqueeze(2).broadcast_to([P, T, C]), ALU.mult).then_inc(y_step, 1)

            def add_y(b):
                g.tensor_tensor(xblk(b), xs[:].rearrange("p t c -> p (t c)"),
                                yn[:].rearrange("p t c -> p (t c)"), ALU.add).then_inc(y_added, 1)

            root(0)
            masks()
            pool.wait_ge(w2h_ready, 1)
            g.tensor_tensor(w2l[:], w2f[:], w2h[:], ALU.subtract).then_inc(w2_split, 1)

            def slot(n, kind):
                if has_pre(kind):
                    root(n + 1)
                low(n, POOL_LO[0])
                if has_kv(kind):
                    y_of(n - 2)
                    pool.wait_ge(y_step, 2 * (n - 1))
                low(n, POOL_LO[1])
                if has_kv(kind):
                    add_y(n - 2)
                for e in POOL_LO[2:4]:
                    low(n, e)
                if has_ln2(kind):
                    second_roots(n - 1)
                if has_kv(kind):
                    pool.wait_ge(q_exp, n - 1)
                low(n, POOL_LO[4])
                if has_kv(kind):
                    g.tensor_tensor(qall[:, bass.ds((n - 2) * NB, NB)], posq[:], expq[:],
                                    ALU.add).then_inc(q_ready, 1)
                low(n, POOL_LO[5])

            run_slots(pool, slot)

        @block.scalar
        def _(act):
            a = nc.scalar
            act.dma_start(gwf[:], gate_w).then_inc(gw_here, 16)
            act.dma_start(b1r[:], b1.rearrange("e (j p) -> (e j) p", p=P)).then_inc(b1_here, 16)
            act.dma_start(gb[:], gate_b.partition_broadcast(P)).then_inc(gb_here, 16)
            act.dma_start(b2r[:], b2).then_inc(b2_here, 16)
            act.dma_start(wqkv[:], w_qkv).then_inc(qkv_here, 16)
            act.dma_start(gam[:], gamma.rearrange("(c a) -> c a", a=1)).then_inc(gam_here, 16)
            act.dma_start(bet[:], beta.rearrange("(c a) -> c a", a=1)).then_inc(bet_here, 16)
            act.dma_start(wout[:], w_out).then_inc(wo_here, 16)

            def spread_gates(s):
                act.wait_ge(wb_ps, s + 1)
                a.activation(wbc[0 if spread_gates.even else 1][:], wb[:], ACT.Copy).then_inc(wbc_ready, 1)

            def high(n, e):
                act.wait_ge(h_ready, n * CH + J * e + J)
                a.activation(hhi[e % RING][:], h32[e % RING][:], ACT.Copy).then_inc(hi_ready, 1)

            def x_high(m, par):
                act.wait_ge(xT_ps, m + 1)
                a.activation(xTh[par][:], tr[:], ACT.Copy).then_inc(xTh_ready, 1)

            def gate_exp(m):
                act.wait_ge(logit_ready, m + 1)
                a.activation(ex[:], lg[:], ACT.Exp).then_inc(exp_ready, 1)

            def gates_T(m, par):
                act.wait_ge(gT_ps, m + 1)
                a.activation(gT[par][:], mi[0:2 * E, 0:NB // 2].bitcast(F16), ACT.Copy).then_inc(gT_ready, 1)

            def out_T(m):
                act.wait_ge(down_done, m * E + E)
                if not (isinstance(m, int) and m == 0):
                    act.wait_ge(o_ps, m)
                a.activation(oT[:], acc[:], ACT.Copy, scale=0.5).then_inc(oT_ready, 1)

            def spread(n, e):
                spread_gates.even = e % 2 == 0
                spread_gates(n * E + e)

            x_high(0, 0)
            act.wait_ge(w1_here[0], 16)
            a.activation(w1h[:, 0:EARLY], w1f[:, 0:EARLY], ACT.Copy).then_inc(w1h_ready, 1)
            gate_exp(0)
            act.wait_ge(w1_here[1], 16)
            a.activation(w1h[:, EARLY:E], w1f[:, EARLY:E], ACT.Copy).then_inc(w1h_ready, 1)
            gates_T(0, 0)
            spread(0, 0)
            act.wait_ge(w2_here, 16)
            a.activation(w2h[:], w2f[:], ACT.Copy).then_inc(w2h_ready, 1)

            def slot(n, kind):
                par = kind % 2
                for e in range(E):
                    if e == LAG and has_post(kind):
                        out_T(n - 1)
                    if e < E - 1:
                        spread(n, e + 1)
                    elif has_pre(kind):
                        spread(n + 1, 0)
                    if e == 4 and has_att(kind):
                        act.wait_ge(attT_ps, n + 3 - NBLK)
                        a.activation(attT[:], tr[:], ACT.Copy).then_inc(attT_ready, 1)
                    if e == 5 and has_pre(kind):
                        gates_T(n + 1, 1 - par)
                    high(n, e)
                    if e == 0 and has_att(kind):
                        act.wait_ge(q_ready, n + 3 - NBLK)
                        if kind > NBLK - 2:
                            act.wait_ge(num_ps, n + 2 - NBLK)
                        a.activation(qcur[:], qall[:, bass.ds((n + 2 - NBLK) * NB, NB)],
                                     ACT.Copy).then_inc(qcur_ready, 1)
                    if e == 0 and has_kv(kind):
                        if kind == 2:
                            act.wait_ge(gam_here, 16)
                            act.wait_ge(bet_here, 16)
                        act.wait_ge(xn2T_ps, n - 1)
                        a.activation(xn2T[:], tr[:], ACT.Identity, bias=bet[:, 0:1],
                                     scale=gam[:, 0:1]).then_inc(xn2T_ready, 1)
                    if e == 1 and has_pre(kind):
                        x_high(n + 1, 1 - par)
                    if e == 2 and has_pre(kind):
                        gate_exp(n + 1)
                    if e == 3 and has_kv(kind):
                        act.wait_ge(k_ps, n - 1)
                        a.activation(negk[:], tr[:], ACT.Relu, scale=-1.0).then_inc(k_neg, 1)
                        a.activation(posk[:], tr[:], ACT.Relu).then_inc(k_pos, 1)
                        act.wait_ge(v_ps, n - 1)
                        a.activation(vone[:, :, 0:C], mi[:].rearrange("p (t c) -> p t c", t=T),
                                     ACT.Copy).then_inc(v_ready, 1)
                        act.wait_ge(k_neg, n - 1)
                        a.activation(expk[:], negk[:], ACT.Exp, scale=-1.0).then_inc(k_exp, 1)
                    if e == 4 and has_kv(kind):
                        act.wait_ge(q_ps, n - 1)
                        a.activation(negq[:], mi[:], ACT.Relu, scale=-1.0).then_inc(q_neg, 1)
                        a.activation(posq[:], mi[:], ACT.Relu).then_inc(q_pos, 1)
                        act.wait_ge(q_neg, n - 1)
                        a.activation(expq[:], negq[:], ACT.Exp, scale=-1.0).then_inc(q_exp, 1)

            run_slots(act, slot)
            out_T(NS - 1)

        @block.vector
        def _(dve):
            v = nc.vector

            def stats(m, tile, s_step, s_ready, st, mv, ve, nm):
                link = chain(dve, s_step, m * STAT_LINKS, STAT_LINKS)
                for t in range(T):
                    last = v.bn_stats(st[:, t, :], tile(t))
                link(last)
                v.tensor_tensor(nm[:], st[:, :, 1], st[:, :, 4], ALU.add)
                for t in range(T):
                    last = v.bn_aggr(mv[:, t, :], st[:, t, :])
                link(last)
                v.tensor_scalar(ve[:], mv[:, :, 1], LN_EPS, None, ALU.add)
                v.tensor_scalar(nm[:], nm[:], -0.5, None, ALU.mult).then_inc(s_ready, 1)

            def first_norm(m, b):
                dve.wait_ge(stat_ready, m + 1)
                dve.wait_ge(rs_ready, m + 1)
                for t in range(T):
                    last = v.tensor_scalar(xn[:, t, :], xtile(b, t), nm[:, t:t + 1], rs[:, t:t + 1],
                                           ALU.add, ALU.mult)
                last.then_inc(xn_ready, 1)

            def second_norm(b):
                dve.wait_ge(r12_ready, b + 1)
                for t in range(T):
                    last = v.tensor_scalar(xn2[:, t, :], xs[:, t, :], nm2[:, t:t + 1], r12[:, t:t + 1],
                                           ALU.add, ALU.mult)
                last.then_inc(xn2_ready, 1)

            def x_low(m, par):
                dve.wait_ge(xTh_ready, m + 1)
                v.tensor_tensor(xTl[par][:], tr[:], xTh[par][:], ALU.subtract).then_inc(xTl_ready, 1)

            def gates_a(m):
                link = chain(dve, top_step, m * TOP_LINKS, TOP_LINKS)
                dve.wait_ge(logit_ps, m + 1)
                link(v.tensor_tensor(lg[:], mi[:, 0:T * E].rearrange("p (t e) -> p t e", t=T),
                                     gb[:].unsqueeze(1).broadcast_to([P, T, E]), ALU.add))
                link(v.tensor_reduce(mx[:], lg[:], AX.X, ALU.max))
                v.tensor_tensor(lg[:], lg[:], mx[:].unsqueeze(2).broadcast_to([P, T, E]),
                                ALU.subtract).then_inc(logit_ready, 1)

            def gates_b(m):
                link = chain(dve, top_step, m * TOP_LINKS + 2, TOP_LINKS - 2)
                dve.wait_ge(exp_ready, m + 1)
                link(v.tensor_reduce(sm[:], ex[:], AX.X, ALU.add))
                link(v.reciprocal(rsm[:], sm[:]))
                link(v.tensor_tensor(pr[:], ex[:], rsm[:].unsqueeze(2).broadcast_to([P, T, E]), ALU.mult))
                other = pr[:].unsqueeze(2).broadcast_to([P, T, E, E])
                own = pr[:].unsqueeze(3).broadcast_to([P, T, E, E])
                v.tensor_tensor(gt[:], other, own, ALU.is_gt)
                link(v.tensor_tensor(eq[:], other, own, ALU.is_equal))
                flat = "p t e j -> p t (e j)"
                link(v.tensor_tensor(eq[:].rearrange(flat), eq[:].rearrange(flat),
                                     tri[:].rearrange("p e j -> p (e j)").unsqueeze(1).broadcast_to([P, T, E * E]),
                                     ALU.mult))
                link(v.tensor_tensor(gt[:], gt[:], eq[:], ALU.add))
                link(v.tensor_reduce(rank[:], gt[:], AX.X, ALU.add))
                link(v.scalar_tensor_tensor(out=gate[:], in0=rank[:], scalar=2.0, in1=pr[:],
                                            op0=ALU.is_lt, op1=ALU.mult))
                link(v.tensor_copy(g16[:, :, 0:E], gate[:]))
                v.tensor_tensor(g16[:, :, E:2 * E], gate[:], g16[:, :, 0:E], ALU.subtract).then_inc(gate_ready, 1)

            def add_out(b, m, first):
                dve.wait_ge(o_ps, m + 1)
                v.tensor_tensor(xs[:].rearrange("p t c -> p (t c)") if first else xblk(b), tr[:], xblk(b),
                                ALU.add).then_inc(x_added, 1)

            def hidden(n, e, j):
                c = J * e + j
                if j == 0:
                    dve.wait_ge(wbc_ready, n * E + e + 1)
                dve.wait_ge(z_ps, n * CH + c + 1)
                v.scalar_tensor_tensor(out=h32[e % RING][:, j * NB:(j + 1) * NB], in0=z[c % ZB][:],
                                       scalar=nb1[:, c:c + 1], in1=wbc[e % 2][:],
                                       op0=ALU.max, op1=ALU.mult).then_inc(h_ready, 1)

            def low(n, e):
                dve.wait_ge(hi_ready, n * E + e + 1)
                v.tensor_tensor(hlo[e % RING][:], h32[e % RING][:], hhi[e % RING][:],
                                ALU.subtract).then_inc(lo_dve, 1)

            dve.wait_ge(gw_here, 16)
            v.tensor_copy(gwh[:], gwf[:]).then_inc(gwh_ready, 1)
            dve.wait_ge(gwh_ready, 1)
            v.tensor_tensor(gwl[:], gwf[:], gwh[:], ALU.subtract).then_inc(gw_split, 1)
            dve.wait_ge(x_here[0], 16)
            stats(0, lambda t: xtile(0, t), stat_step, stat_ready, st, mv, ve, nm)
            dve.wait_ge(cst, 3)
            v.tensor_copy(ident16[:], ident[:]).then_inc(id16_ready, 1)
            for i in range(batches):
                last = v.memset(kvacc[i][:], 0.0)
            last.then_inc(kv_zero, 1)
            first_norm(0, 0)
            x_low(0, 0)
            dve.wait_ge(gb_here, 16)
            gates_a(0)
            dve.wait_ge(w1h_ready, 1)
            v.tensor_tensor(w1l[:, 0:EARLY], w1f[:, 0:EARLY], w1h[:, 0:EARLY], ALU.subtract).then_inc(w1_split, 1)
            dve.wait_ge(cst, 12)
            gates_b(0)
            dve.wait_ge(b1T_ps, 1)
            v.tensor_copy(b1t[:], tr[:, 0:CH]).then_inc(b1_ready, 1)
            v.tensor_scalar(nb1[:], tr[:, 0:CH], -1.0, None, ALU.mult).then_inc(nb1_ready, 1)
            dve.wait_ge(w1h_ready, 2)
            v.tensor_tensor(w1l[:, EARLY:E], w1f[:, EARLY:E], w1h[:, EARLY:E], ALU.subtract).then_inc(w1_split, 1)
            dve.wait_ge(b1_ready, 1)
            dve.wait_ge(cst, 22)
            v.tensor_tensor(b1m[:], cmask[:], b1t[:].unsqueeze(2).broadcast_to([P, CH, 2 * E]),
                            ALU.mult).then_inc(b1_ready, 1)
            dve.wait_ge(nb1_ready, 1)

            def finish_kv(b):
                dve.wait_ge(kv_added, BPB * (b + 1))
                v.tensor_tensor(kvm[b][:], kvacc[b][:, 0:C].rearrange("p (h d) -> p h d", h=NH), hmask[:],
                                ALU.mult)
                v.tensor_scalar(dm[b][:], dmask[:], kvacc[b][:, C:C + 1], None, ALU.mult).then_inc(kvm_ready, 1)

            def slot(n, kind):
                par = kind % 2
                if has_pre(kind):
                    if kind == 2:
                        for b in range(kind + 1, NBLK):
                            dve.wait_ge(x_here[b], 16)
                    elif kind < 2:
                        dve.wait_ge(x_here[kind + 1], 16)
                    nb = n + 1 if kind + 1 < NBLK else n + 1 - NBLK
                    stats(n + 1, lambda t: xtile(nb, t), stat_step, stat_ready, st, mv, ve, nm)
                for e in range(E):
                    if e == 7 and has_att(kind):
                        b = n + 2 - NBLK
                        dve.wait_ge(proj_ps, b + 1)
                        dve.wait_ge(y_added, b + 1)
                        v.tensor_tensor(xblk(b), tr[:], xblk(b), ALU.add).then_inc(x2_added, 1)
                        dve.wait_ge(x2_added, b + 1)
                    hidden(n, e, 0)
                    hidden(n, e, 1)
                    if e - 1 in DVE_LO:
                        low(n, e - 1)
                    if e == 0 and kind == NBLK - 2:
                        finish_kv(0)
                    if e == 0 and has_pre(kind):
                        first_norm(n + 1, nb)
                    if e == 1 and has_pre(kind):
                        x_low(n + 1, 1 - par)
                    if e == 1 and has_att(kind):
                        dve.wait_ge(den_ps, n + 3 - NBLK)
                        v.tensor_scalar(dene[:], mi[:, 0:T * NH].rearrange("p (t h) -> p t h", t=T), DENOM_EPS,
                                        None, ALU.add).then_inc(dene_ready, 1)
                        dve.wait_ge(dene_ready, n + 3 - NBLK)
                        v.reciprocal(rden[:], dene[:]).then_inc(rden_ready, 1)
                    if e == 2 and has_pre(kind):
                        gates_a(n + 1)
                    if e == 2 and has_att(kind):
                        dve.wait_ge(rden_ready, n + 3 - NBLK)
                        dve.wait_ge(num_ps, n + 3 - NBLK)
                        v.tensor_tensor(att[:].rearrange("p t (h d) -> p (t h) d", h=NH),
                                        tr[:].rearrange("p (g d) -> p g d", d=HD),
                                        rden[:].rearrange("p t h -> p (t h)").unsqueeze(2).broadcast_to([P, T * NH, HD]),
                                        ALU.mult).then_inc(att_ready, 1)
                    if e == 3 and has_pre(kind):
                        gates_b(n + 1)
                    if e == 4 and has_kv(kind):
                        dve.wait_ge(k_exp, n - 1)
                        v.tensor_tensor(kph[:].rearrange("p t c -> p (t c)"), posk[:], expk[:],
                                        ALU.add).then_inc(k_ready, 1)
                    if kind == 0 and e == 4:
                        dve.wait_ge(b2_ps, 1)
                        v.tensor_copy(b2h[:], tr[0:2 * E, 0:C]).then_inc(b2h_ready, 1)
                        dve.wait_ge(b2h_ready, 1)
                        v.tensor_tensor(b2l[:], tr[0:2 * E, 0:C], b2h[:], ALU.subtract).then_inc(b2_ready, 1)
                    if e == 5 and has_post(kind):
                        if has_ln2(kind) and kind > 1:
                            dve.wait_ge(y_added, n - 1)
                        add_out(n - 1 if kind - 1 < NBLK else n - 1 - NBLK, n - 1, has_ln2(kind))
                        if has_ln2(kind):
                            dve.wait_ge(x_added, n)
                            stats(n - 1, lambda t: xs[:, t, :], stat2_step, stat2_ready, st2, mv2, ve2, nm2)
                    if e == 7 and has_ln2(kind):
                        second_norm(n - 1)
                    if e == 7 and has_kv(kind):
                        acc_b = 0 if kind < 2 + BPB else 1
                        dve.wait_ge(kv_ps, n - 1)
                        if kind == 2:
                            dve.wait_ge(kv_zero, 1)
                        else:
                            dve.wait_ge(kv_added, n - 2)
                        v.tensor_tensor(kvacc[acc_b][:], mi[:, 0:C + 1], kvacc[acc_b][:],
                                        ALU.add).then_inc(kv_added, 1)
                        if kind == NBLK + 1:
                            finish_kv(1)

            run_slots(dve, slot)
            add_out(NBLK - 1, NS - 1, False)

        @block.tensor
        def _(pe):
            mm = nc.tensor.matmul

            def spread(n, e, par):
                if not (isinstance(n, int) and n == 0 and e == 0):
                    pe.wait_ge(wbc_ready, n * E + e)
                if e == 0:
                    pe.wait_ge(gT_ready, n + 1)
                mm(wb[:], sel[:, e, :], gT[par][:], start=True, stop=True).then_inc(wb_ps, 1)

            def up(n, kind, e, par):
                for j in range(J):
                    c = J * e + j
                    if kind > 0 or c >= ZB:
                        pe.wait_ge(h_ready, n * CH + c + 1 - ZB)
                    zb = z[c % ZB][:]
                    wh, wl = (w[:, e, j * P:(j + 1) * P] for w in (w1h, w1l))
                    mm(zb, wh, xTh[par][:], start=True, stop=False)
                    mm(zb, wh, xTl[par][:], start=False, stop=False)
                    mm(zb, wl, xTh[par][:], start=False, stop=True).then_inc(z_ps, 1)

            def down(n, e, par):
                if e in POOL_LO:
                    pe.wait_ge(lo_pool, n * len(POOL_LO) + POOL_LO.index(e) + 1)
                else:
                    pe.wait_ge(lo_dve, n * len(DVE_LO) + DVE_LO.index(e) + 1)
                if e == 0 and not (isinstance(n, int) and n == 0):
                    pe.wait_ge(oT_ready, n)
                if e == E - 1:
                    mm(acc[:], b2h[:], gT[par][:], start=False, stop=False)
                    mm(acc[:], b2l[:], gT[par][:], start=False, stop=False)
                for j in range(J):
                    c = J * e + j
                    hh, hl = (h[e % RING][:, j * NB:(j + 1) * NB] for h in (hhi, hlo))
                    mm(acc[:], w2h[:, c, :], hh, start=(c == 0), stop=False)
                    mm(acc[:], w2l[:, c, :], hh, start=False, stop=False)
                    last = mm(acc[:], w2h[:, c, :], hl, start=False, stop=(c == CH - 1))
                last.then_inc(down_done, 1)

            def transposes(dst, src, signal):
                for t in range(T):
                    last = nc.tensor.transpose(dst[:, t * P:(t + 1) * P], src(t), ident[:])
                last.then_inc(signal, 1)

            def logits(m, par):
                pe.wait_ge(xTl_ready, m + 1)
                for t in range(T):
                    xh, xl = (x[par][:, t * P:(t + 1) * P] for x in (xTh, xTl))
                    o = mi[:, t * E:(t + 1) * E]
                    mm(o, xh, gwh[:], start=True, stop=False)
                    mm(o, xh, gwl[:], start=False, stop=False)
                    last = mm(o, xl, gwh[:], start=False, stop=True)
                last.then_inc(logit_ps, 1)

            def gates_T(m):
                pe.wait_ge(gate_ready, m + 1)
                o = mi[0:2 * E, 0:NB // 2].bitcast(F16)
                for t in range(T):
                    last = nc.tensor.transpose(o[:, t * P:(t + 1) * P], g16[:, t, :], ident16[:])
                last.then_inc(gT_ps, 1)

            pe.wait_ge(cst, 3)
            pe.wait_ge(xn_ready, 1)
            transposes(tr, lambda t: xn[:, t, :], xT_ps)
            pe.wait_ge(gw_split, 1)
            logits(0, 0)
            pe.wait_ge(b1_here, 16)
            nc.tensor.transpose(tr[:, 0:CH], b1r[:], ident[0:CH, 0:CH]).then_inc(b1T_ps, 1)
            pe.wait_ge(id16_ready, 1)
            pe.wait_ge(w1_split, 1)
            for e in range(EARLY):
                up(0, 0, e, 0)
            gates_T(0)
            pe.wait_ge(cst, 18)
            spread(0, 0, 0)
            pe.wait_ge(w1_split, 2)

            def side(n, kind, e):
                par = kind % 2
                m = n + 2 - NBLK
                b = 0 if kind + 2 - NBLK < BPB else 1
                if e == 0 and has_kv(kind):
                    pe.wait_ge(xn2_ready, n - 1)
                    if has_att(kind - 1):
                        pe.wait_ge(x2_added, m)
                    transposes(tr, lambda t: xn2[:, t, :], xn2T_ps)
                if e == 1 and has_pre(kind):
                    pe.wait_ge(xn_ready, n + 2)
                    if has_kv(kind):
                        pe.wait_ge(xn2T_ready, n - 1)
                    transposes(tr, lambda t: xn[:, t, :], xT_ps)
                if e == 1 and has_att(kind):
                    pe.wait_ge(kvm_ready, b + 1)
                    pe.wait_ge(qcur_ready, m + 1)
                    for t in range(T):
                        last = mm(mi[:, t * NH:(t + 1) * NH], qcur[:, t * P:(t + 1) * P], dm[b][:],
                                  start=True, stop=True)
                    last.then_inc(den_ps, 1)
                if e == 2 and has_pre(kind):
                    if has_att(kind):
                        pe.wait_ge(dene_ready, m + 1)
                    logits(n + 1, 1 - par)
                if e == 2 and has_att(kind):
                    pe.wait_ge(xTl_ready, n + 2)
                    for t in range(T):
                        last = mm(tr[:, t * C:(t + 1) * C], qcur[:, t * P:(t + 1) * P],
                                  kvm[b][:].rearrange("p h d -> p (h d)"), start=True, stop=True)
                    last.then_inc(num_ps, 1)
                if e == 3 and has_kv(kind):
                    if has_att(kind):
                        pe.wait_ge(att_ready, m + 1)
                    else:
                        pe.wait_ge(xTl_ready, n + 2)
                    for t in range(T):
                        last = mm(tr[:, t * C:(t + 1) * C], xn2T[:, t * P:(t + 1) * P], wqkv[:, C:2 * C],
                                  start=True, stop=True)
                    last.then_inc(k_ps, 1)
                    pe.wait_ge(logit_ready, n + 2)
                    for t in range(T):
                        last = mm(mi[:, t * C:(t + 1) * C], xn2T[:, t * P:(t + 1) * P], wqkv[:, 2 * C:3 * C],
                                  start=True, stop=True)
                    last.then_inc(v_ps, 1)
                if e == 4 and has_att(kind):
                    pe.wait_ge(att_ready, m + 1)
                    if has_kv(kind):
                        pe.wait_ge(k_pos, n - 1)
                    transposes(tr, lambda t: att[:, t, :], attT_ps)
                if e == 4 and has_kv(kind):
                    pe.wait_ge(v_ready, n - 1)
                    mm(mi[:], wqkv[:, 0:C], xn2T[:], start=True, stop=True).then_inc(q_ps, 1)
                if e == 4 and kind == 0:
                    pe.wait_ge(b1_ready, 2)
                    pe.wait_ge(b2_here, 16)
                    pe.wait_ge(xTl_ready, 2)
                    o = tr[0:2 * E, 0:C]
                    mm(o, idup[:], b2r[:], start=True, stop=False)
                    for c in range(CH):
                        last = mm(o, b1m[:, c, :], w2f[:, c, :], start=False, stop=(c == CH - 1))
                    last.then_inc(b2_ps, 1)
                if e == 5 and has_post(kind):
                    pe.wait_ge(oT_ready, n)
                    if has_att(kind):
                        pe.wait_ge(attT_ready, m + 1)
                    elif has_kv(kind):
                        pe.wait_ge(k_pos, n - 1)
                    elif has_pre(kind):
                        pe.wait_ge(xTl_ready, n + 2)
                    else:
                        pe.wait_ge(x_added, n - 1)
                    transposes(tr, lambda t: oT[:, t * P:(t + 1) * P], o_ps)
                if e == 5 and has_pre(kind):
                    if has_kv(kind):
                        pe.wait_ge(q_pos, n - 1)
                    gates_T(n + 1)
                if e == 6 and has_att(kind):
                    pe.wait_ge(attT_ready, m + 1)
                    pe.wait_ge(x_added, n)
                    for t in range(T):
                        last = mm(tr[:, t * C:(t + 1) * C], attT[:, t * P:(t + 1) * P], wout[:],
                                  start=True, stop=True)
                    last.then_inc(proj_ps, 1)
                if e == 6 and has_kv(kind):
                    pe.wait_ge(k_ready, n - 1)
                    pe.wait_ge(v_ready, n - 1)
                    pe.wait_ge(gT_ready, n + 2)
                    for t in range(T):
                        last = mm(mi[:, 0:C + 1], kph[:, t, :], vone[:, t, :], start=(t == 0), stop=(t == T - 1))
                    last.then_inc(kv_ps, 1)

            def slot(n, kind):
                par = kind % 2
                if kind == 1:
                    pe.wait_ge(qkv_here, 16)
                    pe.wait_ge(wo_here, 16)
                    pe.wait_ge(b2_ready, 1)
                for e in range(E):
                    if e < E - 1:
                        spread(n, e + 1, par)
                    elif has_pre(kind):
                        spread(n + 1, 0, 1 - par)
                    if kind > 0 or e >= EARLY:
                        up(n, kind, e, par)
                    if e != 1:
                        side(n, kind, e)
                    if kind == 0 and e == LAG:
                        pe.wait_ge(w2_split, 1)
                    if e >= LAG:
                        down(n, e - LAG, par)
                    elif kind > 0:
                        down(n - 1, E + e - LAG, 1 - par)
                    if e == 1:
                        side(n, kind, e)

            run_slots(pe, slot)
            for e in range(E - LAG, E):
                down(NS - 1, e, (NS - 1) % 2)
            pe.wait_ge(oT_ready, NS)
            pe.wait_ge(x_added, NS - 1)
            transposes(tr, lambda t: oT[:, t * P:(t + 1) * P], o_ps)


_INS = ['L0_attn_x', 'L0_attn_gamma', 'L0_attn_beta', 'L0_attn_Wqkv', 'L0_attn_Wout', 'L0_ffn_gate_w',
        'L0_ffn_gate_b', 'L0_ffn_w1', 'L0_ffn_b1', 'L0_ffn_w2', 'L0_ffn_b2']
_OUTS = [((2, 2048, 128), 'float32')]


def kernel(**inputs):
    import numpy as _np
    import concourse.bacc as _bacc
    from concourse import mybir as _mybir
    from concourse.bass_utils import run_bass_kernel_spmd as _run

    nc = _bacc.Bacc("TRN2", target_bir_lowering=False, num_devices=1)
    arrays, args = {}, []
    for name in _INS:
        a = _np.ascontiguousarray(inputs[name])
        arrays[f"in_{name}_dram"] = a
        args.append(nc.dram_tensor(f"in_{name}_dram", a.shape, _mybir.dt.from_np(a.dtype), kind="ExternalInput").ap())
    for i, (shape, dtype) in enumerate(_OUTS):
        dt = _mybir.dt.from_np(_np.dtype(dtype))
        args.append(nc.dram_tensor(f"out_{i}_dram", shape, dt, kind="ExternalOutput").ap())
    macaron_block(nc, *args)
    r = _run(nc, [arrays], core_ids=[0])
    got = tuple(r.results[0][f"out_{i}_dram"] for i in range(len(_OUTS)))
    return got[0]
```

```python
from contextlib import ExitStack

import concourse.bass as bass
from concourse import mybir

F32 = mybir.dt.float32
F16 = mybir.dt.float16
ALU = mybir.AluOpType
ACT = mybir.ActivationFunctionType
AX = mybir.AxisListType

P = 128
C = 128
T = 4
NB = T * P
E = 8
J = 2
CH = E * J
NH = 16
HD = C // NH
LAG = 3
ZB = 4
RING = 4
EB = 2
EARLY = 2
LN_EPS = 1e-5
DENOM_EPS = 1e-6
KV_SCALE = 2.0 ** -4
POOL_LO = (0, 1, 2, 4, 6, 7)
DVE_LO = (3, 5)
W1_CUT = 5
W2_HALVES = (slice(0, CH // 2), slice(CH // 2, CH))
GR = 3 * E * T
STAT_LINKS = 2
TOP_LINKS = 10
LN2_LINKS = 5


def macaron_block(nc, x_in, gamma, beta, w_qkv, w_out, gate_w, gate_b, w1, b1, w2, b2, out):
    batches, seq, _ = x_in.shape
    NBLK = batches * seq // NB
    NS = 2 * NBLK
    BPB = NBLK // batches
    assert (NBLK, BPB, batches) == (8, 4, 2) and w1.shape == (E, C, J * P)
    x_dram = x_in.rearrange("b (n p t) c -> (b n) p (t c)", p=P, t=T)
    out_dram = out.rearrange("b (n p t) c -> (b n) p (t c)", p=P, t=T)
    gate_dram = [nc.dram_tensor(f"gates{i}", [E * T, P], F32).ap() for i in range(2)]

    with ExitStack() as ctx:
        def sb(name, shape, dt=F32):
            return ctx.enter_context(nc.sbuf_tensor(name, shape, dt))

        def bank(name):
            return ctx.enter_context(nc.psum_tensor(name, [P, 512], F32))

        def sem(name):
            return ctx.enter_context(nc.semaphore(name))

        z = [bank(f"z{i}") for i in range(ZB)]
        acc = bank("acc")
        tr, mi, aux = bank("tr"), bank("mi"), bank("aux")

        xres = sb("xres", [P, NBLK * T * C])
        w1f = sb("w1f", [P, E, J * P])
        w1h = sb("w1h", [P, E, J * P], F16)
        w1l = sb("w1l", [P, E, J * P], F16)
        w2f = sb("w2f", [P, CH, C])
        w2h = sb("w2h", [P, CH, C], F16)
        w2l = sb("w2l", [P, CH, C], F16)
        gwf = sb("gwf", [P, E])
        gwh = sb("gwh", [P, E], F16)
        gwl = sb("gwl", [P, E], F16)
        gb = sb("gb", [P, E])
        wqkv = sb("wqkv", [P, 3 * C])
        wqkvh = sb("wqkvh", [P, 3 * C], F16)
        wqkvl = sb("wqkvl", [P, 3 * C], F16)
        wout = sb("wout", [P, C])
        wouth = sb("wouth", [P, C], F16)
        woutl = sb("woutl", [P, C], F16)
        gam = sb("gam", [P, 1])
        bet = sb("bet", [P, 1])
        b1r = sb("b1r", [CH, P])
        nb1 = sb("nb1", [P, CH])
        b1h = sb("b1h", [P, CH], F16)
        b1l = sb("b1l", [P, CH], F16)
        b2r = sb("b2r", [E, C])
        b2h = sb("b2h", [C, E], F16)
        b2t = sb("b2t", [C, E])
        b2s = sb("b2s", [C, T, 3, E, T])
        b2x = sb("b2x", [GR, T, C], F16)
        ident = sb("ident", [P, P])
        tri = sb("tri", [P, E, E])
        hmask = sb("hmask", [P, NH, HD])
        dmask = sb("dmask", [P, NH])
        sel = sb("sel", [2 * E * T, EARLY * T, P], F16)
        nhalf = sb("nhalf", [P, T])
        epst = sb("epst", [P, T])
        st = sb("st", [P, T, 6])
        mv = sb("mv", [P, T, 2])
        ve = sb("ve", [P, T])
        nm = sb("nm", [P, T])
        rs = sb("rs", [P, T])
        xn = sb("xn", [P, T, C])
        xTh = [sb(f"xTh{i}", [P, NB], F16) for i in range(2)]
        xTl = [sb(f"xTl{i}", [P, NB], F16) for i in range(2)]
        lg = sb("lg", [P, T, E])
        mx = sb("mx", [P, T])
        ex = sb("ex", [P, T, E])
        sm = sb("sm", [P, T])
        rsm = sb("rsm", [P, T])
        pr = sb("pr", [P, T, E])
        gt = sb("gt", [P, T, E, E])
        eq = sb("eq", [P, T, E, E])
        rank = sb("rank", [P, T, E])
        gate = sb("gate", [P, 3, E, T])
        gateh = sb("gateh", [P, E, T], F16)
        gT = [sb(f"gT{i}", [E * T, P]) for i in range(2)]
        g3 = [sb(f"g3_{i}", [GR, P], F16) for i in range(2)]
        wbc = [sb(f"wbc{i}", [P, E, NB]) for i in range(2)]
        h32 = [sb(f"h32_{i}", [P, J * NB]) for i in range(RING)]
        hhi = [sb(f"hhi{i}", [P, J * NB], F16) for i in range(RING)]
        hlo = [sb(f"hlo{i}", [P, J * NB], F16) for i in range(RING)]
        oT = sb("oT", [P, NB])
        st2 = sb("st2", [P, T, 6])
        mv2 = sb("mv2", [P, T, 2])
        ve2 = sb("ve2", [P, T])
        nm2 = sb("nm2", [P, T])
        r1 = sb("r1", [P, T])
        r1s = sb("r1s", [P, T])
        vy = sb("vy", [P, T])
        vye = sb("vye", [P, T])
        r2 = sb("r2", [P, T])
        r12 = sb("r12", [P, T])
        xs = sb("xs", [P, T, C])
        yc = sb("yc", [P, T, C])
        yn = sb("yn", [P, T, C])
        xn2 = sb("xn2", [P, T, C])
        xn2T = sb("xn2T", [P, NB])
        xn2Th = sb("xn2Th", [P, NB], F16)
        xn2Tl = sb("xn2Tl", [P, NB], F16)
        negq = sb("negq", [P, NB])
        expq = sb("expq", [P, NB])
        negk = sb("negk", [P, NB])
        expk = sb("expk", [P, NB])
        posk = sb("posk", [P, NB])
        posq = sb("posq", [P, NB])
        kph = sb("kph", [P, T, C])
        vone = sb("vone", [P, T, C + 1])
        qall = sb("qall", [P, NBLK * NB])
        qh = sb("qh", [P, NB], F16)
        ql = sb("ql", [P, NB], F16)
        kvacc = [sb(f"kvacc{i}", [P, C + 1]) for i in range(batches)]
        kvd = [sb(f"kvd{i}", [P, C + NH]) for i in range(batches)]
        kvdh = [sb(f"kvdh{i}", [P, C + NH], F16) for i in range(batches)]
        kvdl = [sb(f"kvdl{i}", [P, C + NH], F16) for i in range(batches)]
        dene = sb("dene", [P, T, NH])
        rden = sb("rden", [P, T, NH])
        att = sb("att", [P, T, C])
        attT = sb("attT", [P, NB])
        attTh = sb("attTh", [P, NB], F16)
        attTl = sb("attTl", [P, NB], F16)

        def xblk(b):
            return xres[:, bass.ds(b * (T * C), T * C)]

        def out_blk(b):
            return out_dram[b] if isinstance(b, int) else out_dram[bass.ds(b, 1)].rearrange("a p c -> (a p) c")

        HALVES = (slice(0, NB // 2), slice(NB // 2, NB))

        def nd_tiles(nd):
            return nd[:, 0:2 * (C + NH)].rearrange("p (t c) -> p t c", t=2)

        def xtile(b, t):
            return xres[:, bass.ds(b * (T * C) + t * C, C)]

        x_here = [sem(f"x_here{i}") for i in range(NBLK)]
        gw_here, gb_here, b1_here = sem("gw_here"), sem("gb_here"), sem("b1_here")
        w1_here = [sem("w1_here0"), sem("w1_here1")]
        w2_here, b2_here, qkv_here, wo_here = sem("w2_here"), sem("b2_here"), sem("qkv_here"), sem("wo_here")
        gam_here, bet_here = sem("gam_here"), sem("bet_here")
        cst = sem("cst")
        gw_split, w1_split, w2_split = sem("gw_split"), sem("w1_split"), sem("w2_split")
        w1_split_pool = sem("w1_split_pool")
        w2h_ready, gwh_ready, w1h_ready = sem("w2h_ready"), sem("gwh_ready"), sem("w1h_ready")
        b1T_ps, b1_ready, b1_split = sem("b1T_ps"), sem("b1_ready"), sem("b1_split")
        b2T_ps, b2_parts, b2T_ready = sem("b2T_ps"), sem("b2_parts"), sem("b2T_ready")
        b2_ps, b2_ready = sem("b2_ps"), sem("b2_ready")
        kv_zero, b2_zero = sem("kv_zero"), sem("b2_zero")
        spread_ps, spread_ready = sem("spread_ps"), sem("spread_ready")
        gates_out = sem("gates_out")
        wbc_here = [[sem(f"wbc{k}_here{i}") for i in range(E // EB)] for k in range(2)]
        z_ps, h_ready, hi_ready = sem("z_ps"), sem("h_ready"), sem("hi_ready")
        lo_pool, lo_dve, down_done = sem("lo_pool"), sem("lo_dve"), sem("down_done")
        stat_step, stat_ready = sem("stat_step"), sem("stat_ready")
        rs_ready, xn_ready = sem("rs_ready"), sem("xn_ready")
        xn_half, xT_half, xTh_half = sem("xn_half"), sem("xT_half"), sem("xTh_half")
        xT_ps, xTh_ready, xTl_ready = sem("xT_ps"), sem("xTh_ready"), sem("xTl_ready")
        logit_ps, logit_ready, exp_ready = sem("logit_ps"), sem("logit_ready"), sem("exp_ready")
        rank_ready, g3_ready = sem("rank_ready"), sem("g3_ready")
        top_step, gate_ready, gT_ps, gT_ready = sem("top_step"), sem("gate_ready"), sem("gT_ps"), sem("gT_ready")
        oT_ready, o_ps, x_added = sem("oT_ready"), sem("o_ps"), sem("x_added")
        stored = sem("stored")
        stat2_step, stat2_ready, ln2_step = sem("stat2_step"), sem("stat2_ready"), sem("ln2_step")
        xn2_ready, y_step, y_added = sem("xn2_ready"), sem("y_step"), sem("y_added")
        r12_ready = sem("r12_ready")
        qkv_high, qkv_split, wo_high, wo_split = sem("qkv_high"), sem("qkv_split"), sem("wo_high"), sem("wo_split")
        xn2T_ps, xn2T_ready, xn2Tl_ready = sem("xn2T_ps"), sem("xn2T_ready"), sem("xn2Tl_ready")
        q_ps, q_neg, q_pos, q_exp, q_ready = sem("q_ps"), sem("q_neg"), sem("q_pos"), sem("q_exp"), sem("q_ready")
        k_ps, k_neg, k_pos, k_exp, k_ready = sem("k_ps"), sem("k_neg"), sem("k_pos"), sem("k_exp"), sem("k_ready")
        v_ps, v_ready, kv_ps, kv_added = sem("v_ps"), sem("v_ready"), sem("kv_ps"), sem("kv_added")
        kvd_ready = sem("kvd_ready")
        kvd_step, qh_ready, ql_ready = sem("kvd_step"), sem("qh_ready"), sem("ql_ready")
        attTl_ready = sem("attTl_ready")
        dene_ready, rden_ready = sem("dene_ready"), sem("rden_ready")
        num_ps, att_ready, attT_ps, attT_ready = sem("num_ps"), sem("att_ready"), sem("attT_ps"), sem("attT_ready")
        proj_ps, x2_added = sem("proj_ps"), sem("x2_added")

        def has_post(n):
            return n >= 1

        def has_ln2(n):
            return 1 <= n <= NBLK

        def has_kv(n):
            return 2 <= n <= NBLK + 1

        def has_att(n):
            return NBLK - 2 <= n <= NS - 3

        def has_pre(n):
            return n <= NS - 2

        LOOPS = {2: 6, NBLK + 2: NS - 2}

        def run_slots(eng, slot):
            n = 0
            while n < NS:
                if n in LOOPS:
                    with eng.Fori(0, (LOOPS[n] - n) // 2) as i:
                        slot(i * 2 + n, n)
                        slot(i * 2 + (n + 1), n + 1)
                    n = LOOPS[n]
                else:
                    slot(n, n)
                    n += 1

        def chain(eng, s, base, links):
            count = [0]

            def link(ins):
                count[0] += 1
                assert count[0] <= links
                ins.then_inc(s, 1)
                eng.wait_ge(s, base + count[0])
            return link

        block = ctx.enter_context(nc.Block())

        @block.sync
        def _(sp):
            sp.dma_start(xblk(0), x_dram[0]).then_inc(x_here[0], 16)
            w1_dram = w1.rearrange("e c h -> c e h")
            sp.dma_start(w1f[:, 0:EARLY], w1_dram[:, 0:EARLY]).then_inc(w1_here[0], 16)
            sp.dma_start(xblk(1), x_dram[1]).then_inc(x_here[1], 16)
            sp.dma_start(w1f[:, EARLY:E], w1_dram[:, EARLY:E]).then_inc(w1_here[1], 16)
            sp.dma_start(w2f[:], w2.rearrange("e (j p) c -> p (e j) c", p=P)).then_inc(w2_here, 16)
            sp.dma_start(xblk(2), x_dram[2]).then_inc(x_here[2], 16)
            sp.dma_start(wqkv[:], w_qkv).then_inc(qkv_here, 16)
            sp.dma_start(gam[:], gamma.rearrange("(c a) -> c a", a=1)).then_inc(gam_here, 16)
            sp.dma_start(bet[:], beta.rearrange("(c a) -> c a", a=1)).then_inc(bet_here, 16)
            sp.dma_start(wout[:], w_out).then_inc(wo_here, 16)

            def spread_gates(m, par, groups):
                sp.wait_ge(gT_ready, m + 1)
                sp.dma_start(gate_dram[par], gT[par][:]).then_inc(gates_out, 16)
                sp.wait_ge(gates_out, m * 16 + 16)
                for i in groups:
                    src = gate_dram[par][i * EB * T:(i + 1) * EB * T].rearrange("r p -> (r p)").partition_broadcast(P)
                    sp.dma_start(wbc[par][:, i * EB:(i + 1) * EB, :].rearrange("p e n -> p (e n)"),
                                 src).then_inc(wbc_here[par][i], 16)

            def store(b):
                sp.wait_ge(x_added, b + (NBLK + 1))
                sp.dma_start(out_blk(b), xblk(b)).then_inc(stored, 16)

            def slot(n, kind):
                if has_pre(kind):
                    spread_gates(n + 1, 1 - kind % 2, range(E // EB))
                if has_post(kind) and not has_ln2(kind):
                    store(n - 1 - NBLK)

            spread_gates(0, 0, range(EARLY // EB, E // EB))
            for b in range(3, NBLK):
                sp.dma_start(xblk(b), x_dram[b]).then_inc(x_here[b], 16)
            run_slots(sp, slot)
            for i, half in enumerate(HALVES):
                sp.wait_ge(x_added, NS + i)
                sp.dma_start(out_blk(NBLK - 1)[:, half], xblk(NBLK - 1)[:, half]).then_inc(stored, 16)
            sp.wait_ge(stored, 16 * (NBLK + 1))

        @block.gpsimd
        def _(pool):
            g = nc.gpsimd
            g.memset(nhalf[:], -0.5).then_inc(cst, 1)
            g.memset(ident[:], 0.0).then_inc(cst, 1)
            pool.wait_ge(cst, 2)
            g.affine_select(out=ident[:], in_=ident[:], compare_op=ALU.not_equal, fill=1.0, base=0,
                            pattern=[[-1, P]], channel_multiplier=1).then_inc(cst, 1)

            def masks():
                g.memset(tri[:], 1.0).then_inc(cst, 1)
                g.memset(sel[:], 0.0).then_inc(cst, 1)
                g.memset(hmask[:], KV_SCALE).then_inc(cst, 1)
                g.memset(dmask[:], KV_SCALE).then_inc(cst, 1)
                g.memset(epst[:], LN_EPS).then_inc(cst, 1)
                g.memset(vone[:], 1.0).then_inc(cst, 1)
                pool.wait_ge(cst, 9)
                g.affine_select(out=tri[:], in_=tri[:], compare_op=ALU.is_ge, fill=0.0, base=-1,
                                pattern=[[1, E], [-1, E]], channel_multiplier=0).then_inc(cst, 1)
                g.affine_select(out=sel[:], in_=sel[:], compare_op=ALU.not_equal, fill=1.0, base=0,
                                pattern=[[-1, EARLY * T], [0, P]], channel_multiplier=1).then_inc(cst, 1)
                g.affine_select(out=hmask[:], in_=hmask[:], compare_op=ALU.is_ge, fill=0.0, base=0,
                                pattern=[[-HD, NH], [0, HD]], channel_multiplier=1).then_inc(cst, 1)
                g.affine_select(out=dmask[:], in_=dmask[:], compare_op=ALU.is_ge, fill=0.0, base=0,
                                pattern=[[-HD, NH]], channel_multiplier=1).then_inc(cst, 1)
                pool.wait_ge(cst, 13)
                g.affine_select(out=sel[:], in_=sel[:], compare_op=ALU.not_equal, fill=1.0, base=-E * T,
                                pattern=[[-1, EARLY * T], [0, P]], channel_multiplier=1).then_inc(cst, 1)
                g.affine_select(out=hmask[:], in_=hmask[:], compare_op=ALU.is_ge, fill=0.0, base=HD - 1,
                                pattern=[[HD, NH], [0, HD]], channel_multiplier=-1).then_inc(cst, 1)
                g.affine_select(out=dmask[:], in_=dmask[:], compare_op=ALU.is_ge, fill=0.0, base=HD - 1,
                                pattern=[[HD, NH]], channel_multiplier=-1).then_inc(cst, 1)

            def root(m):
                pool.wait_ge(stat_ready, m + 1)
                g.tensor_tensor(rs[:], ve[:], nhalf[:], ALU.pow).then_inc(rs_ready, 1)

            def low(n, e):
                pool.wait_ge(hi_ready, n * E + e + 1)
                g.tensor_tensor(hlo[e % RING][:], h32[e % RING][:], hhi[e % RING][:],
                                ALU.subtract).then_inc(lo_pool, 1)

            def second_roots(b):
                link = chain(pool, ln2_step, b * LN2_LINKS, LN2_LINKS)
                pool.wait_ge(stat2_ready, b + 1)
                link(g.tensor_tensor(r1[:], ve2[:], nhalf[:], ALU.pow))
                link(g.tensor_tensor(r1s[:], r1[:], r1[:], ALU.mult))
                link(g.tensor_tensor(vy[:], r1s[:], mv2[:, :, 1], ALU.mult))
                link(g.tensor_tensor(vye[:], vy[:], epst[:], ALU.add))
                link(g.tensor_tensor(r2[:], vye[:], nhalf[:], ALU.pow))
                g.tensor_tensor(r12[:], r1[:], r2[:], ALU.mult).then_inc(r12_ready, 1)

            def y_of(b):
                g.tensor_tensor(yc[:], xs[:], nm2[:].unsqueeze(2).broadcast_to([P, T, C]), ALU.add).then_inc(y_step, 1)
                pool.wait_ge(y_step, 2 * b + 1)
                g.tensor_tensor(yn[:], yc[:], r1[:].unsqueeze(2).broadcast_to([P, T, C]), ALU.mult).then_inc(y_step, 1)

            def add_y(b):
                g.tensor_tensor(xblk(b), xs[:].rearrange("p t c -> p (t c)"),
                                yn[:].rearrange("p t c -> p (t c)"), ALU.add).then_inc(y_added, 1)

            root(0)
            masks()
            root(1)
            g.memset(b2s[:], 0.0).then_inc(b2_zero, 1)
            pool.wait_ge(w1h_ready, 2)
            g.tensor_tensor(w1l[:, W1_CUT:E], w1f[:, W1_CUT:E], w1h[:, W1_CUT:E],
                            ALU.subtract).then_inc(w1_split_pool, 1)
            for i, half in enumerate(W2_HALVES):
                pool.wait_ge(w2h_ready, i + 1)
                g.tensor_tensor(w2l[:, half], w2f[:, half], w2h[:, half], ALU.subtract).then_inc(w2_split, 1)

            def slot(n, kind):
                if has_att(kind):
                    pool.wait_ge(qh_ready, n + 3 - NBLK)
                if kind > 0:
                    low(n - 1, POOL_LO[5])
                if has_att(kind):
                    g.tensor_tensor(ql[:], qall[:, bass.ds((n + 2 - NBLK) * NB, NB)], qh[:],
                                    ALU.subtract).then_inc(ql_ready, 1)
                low(n, POOL_LO[0])
                if has_kv(kind):
                    pool.wait_ge(xn2T_ready, n - 1)
                    g.tensor_tensor(xn2Tl[:], xn2T[:], xn2Th[:], ALU.subtract).then_inc(xn2Tl_ready, 1)
                    y_of(n - 2)
                    pool.wait_ge(y_step, 2 * (n - 1))
                low(n, POOL_LO[1])
                if has_kv(kind):
                    add_y(n - 2)
                if kind + 2 < NBLK:
                    root(n + 2)
                low(n, POOL_LO[2])
                if has_att(kind):
                    pool.wait_ge(attT_ready, n + 3 - NBLK)
                    g.tensor_tensor(attTl[:], attT[:], attTh[:], ALU.subtract).then_inc(attTl_ready, 1)
                low(n, POOL_LO[3])
                if kind == 1:
                    pool.wait_ge(qkv_high, 1)
                    g.tensor_tensor(wqkvl[:], wqkv[:], wqkvh[:], ALU.subtract).then_inc(qkv_split, 1)
                    pool.wait_ge(wo_high, 1)
                    g.tensor_tensor(woutl[:], wout[:], wouth[:], ALU.subtract).then_inc(wo_split, 1)
                    for i in range(batches):
                        last = g.memset(kvacc[i][:], 0.0)
                    last.then_inc(kv_zero, 1)
                if has_ln2(kind):
                    second_roots(n - 1)
                if kind == 0:
                    pool.wait_ge(b2_parts, 1)
                    for t in range(T):
                        last = g.tensor_tensor(b2s[:, t, 2, :, t], b2t[:], b2h[:], ALU.subtract)
                    last.then_inc(b2T_ready, 1)
                if has_kv(kind):
                    pool.wait_ge(q_exp, n - 1)
                low(n, POOL_LO[4])
                if has_kv(kind):
                    g.tensor_tensor(qall[:, bass.ds((n - 2) * NB, NB)], posq[:], expq[:],
                                    ALU.add).then_inc(q_ready, 1)
                if has_pre(kind + 1) and kind + 2 >= NBLK:
                    root(n + 2)

            run_slots(pool, slot)

        @block.scalar
        def _(act):
            a = nc.scalar
            act.dma_start(gwf[:], gate_w).then_inc(gw_here, 16)
            act.dma_start(b1r[:], b1.rearrange("e (j p) -> (e j) p", p=P)).then_inc(b1_here, 16)
            act.dma_start(gb[:], gate_b.partition_broadcast(P)).then_inc(gb_here, 16)
            act.dma_start(b2r[:], b2).then_inc(b2_here, 16)

            def high(n, e):
                act.wait_ge(h_ready, n * CH + J * e + J)
                a.activation(hhi[e % RING][:], h32[e % RING][:], ACT.Copy).then_inc(hi_ready, 1)

            def x_high(m, par):
                act.wait_ge(xT_ps, m + 1)
                a.activation(xTh[par][:], tr[:], ACT.Copy).then_inc(xTh_ready, 1)

            def gate_exp(m):
                act.wait_ge(logit_ready, m + 1)
                a.activation(ex[:], lg[:], ACT.Exp).then_inc(exp_ready, 1)

            def gates_T(m, par):
                act.wait_ge(gT_ps, m + 1)
                a.activation(gT[par][:], aux[0:E * T, 0:P], ACT.Copy).then_inc(gT_ready, 1)
                a.activation(g3[par][:], aux[0:GR, 0:P], ACT.Copy).then_inc(g3_ready, 1)

            def out_T(m):
                act.wait_ge(down_done, m * E + E)
                if not (isinstance(m, int) and m == 0):
                    act.wait_ge(o_ps, m)
                a.activation(oT[:], acc[:], ACT.Copy, scale=0.5).then_inc(oT_ready, 1)

            act.wait_ge(w1_here[0], 16)
            a.activation(w1h[:, 0:EARLY], w1f[:, 0:EARLY], ACT.Copy).then_inc(w1h_ready, 1)
            for half, bank_i, there, done in zip(HALVES, (tr, mi), (xT_half, xT_ps), (xTh_half, xTh_ready)):
                act.wait_ge(there, 1)
                a.activation(xTh[0][:, half], bank_i[:, half], ACT.Copy).then_inc(done, 1)
            gate_exp(0)
            act.wait_ge(w1_here[1], 16)
            a.activation(w1h[:, EARLY:E], w1f[:, EARLY:E], ACT.Copy).then_inc(w1h_ready, 1)
            act.wait_ge(w2_here, 16)
            for half in W2_HALVES:
                a.activation(w2h[:, half], w2f[:, half], ACT.Copy).then_inc(w2h_ready, 1)
            gates_T(0, 0)
            for e in range(EARLY):
                act.wait_ge(spread_ps, e + 1)
                a.activation(wbc[0][:, e, :], (acc, mi)[e][:], ACT.Copy).then_inc(spread_ready, 1)

            def slot(n, kind):
                par = kind % 2
                if kind == 0:
                    x_high(1, 1)
                for e in range(E):
                    if e == 1 and has_pre(kind) and kind > 0:
                        x_high(n + 1, 1 - par)
                    if e == LAG - 1 and has_post(kind):
                        out_T(n - 1)
                    if e == 4 and has_att(kind):
                        act.wait_ge(attT_ps, n + 3 - NBLK)
                        a.activation(attT[:], mi[:], ACT.Copy)
                        a.activation(attTh[:], mi[:], ACT.Copy).then_inc(attT_ready, 1)
                    if e == 5 and has_pre(kind):
                        gates_T(n + 1, 1 - par)
                    if e == 5 and kind == 0:
                        act.wait_ge(b2T_ps, 1)
                        act.wait_ge(b2_zero, 1)
                        a.activation(b2t[:], mi[:, 0:E], ACT.Copy)
                        a.activation(b2h[:], mi[:, 0:E], ACT.Copy)
                        for t in range(T):
                            last = a.activation(b2s[:, t, 0:2, :, t], mi[:, 0:E].unsqueeze(1).broadcast_to([C, 2, E]),
                                                ACT.Copy)
                        last.then_inc(b2_parts, 1)
                    if e == 0 and has_att(kind):
                        act.wait_ge(q_ready, n + 3 - NBLK)
                        if kind > NBLK - 2:
                            act.wait_ge(num_ps, n + 2 - NBLK)
                        a.activation(qh[:], qall[:, bass.ds((n + 2 - NBLK) * NB, NB)],
                                     ACT.Copy).then_inc(qh_ready, 1)
                    if e == 0 and has_kv(kind):
                        if kind == 2:
                            act.wait_ge(gam_here, 16)
                            act.wait_ge(bet_here, 16)
                        act.wait_ge(xn2T_ps, n - 1)
                        a.activation(xn2T[:], tr[:], ACT.Identity, bias=bet[:, 0:1], scale=gam[:, 0:1])
                        a.activation(xn2Th[:], tr[:], ACT.Identity, bias=bet[:, 0:1],
                                     scale=gam[:, 0:1]).then_inc(xn2T_ready, 1)
                    if e == 7 and kind == 0:
                        act.wait_ge(b2_ps, 1)
                        a.activation(b2x[:].rearrange("r t c -> r (t c)"), mi[0:GR, :], ACT.Copy).then_inc(b2_ready, 1)
                    if e == 3 and kind == 1:
                        act.wait_ge(qkv_here, 16)
                        a.activation(wqkvh[:], wqkv[:], ACT.Copy).then_inc(qkv_high, 1)
                        act.wait_ge(wo_here, 16)
                        a.activation(wouth[:], wout[:], ACT.Copy).then_inc(wo_high, 1)
                    high(n, e)
                    if e == 3 and has_pre(kind):
                        gate_exp(n + 1)
                    if e == 3 and has_kv(kind):
                        act.wait_ge(v_ps, n - 1)
                        a.activation(vone[:, :, 0:C], mi[:].rearrange("p (t c) -> p t c", t=T),
                                     ACT.Copy).then_inc(v_ready, 1)
                        act.wait_ge(k_ps, n - 1)
                        a.activation(negk[:], tr[:], ACT.Relu, scale=-1.0).then_inc(k_neg, 1)
                        a.activation(posk[:], tr[:], ACT.Relu).then_inc(k_pos, 1)
                        act.wait_ge(k_neg, n - 1)
                        a.activation(expk[:], negk[:], ACT.Exp, scale=-1.0).then_inc(k_exp, 1)
                    if e == 4 and has_kv(kind):
                        act.wait_ge(q_ps, n - 1)
                        a.activation(negq[:], tr[:], ACT.Relu, scale=-1.0).then_inc(q_neg, 1)
                        a.activation(posq[:], tr[:], ACT.Relu).then_inc(q_pos, 1)
                        act.wait_ge(q_neg, n - 1)
                        a.activation(expq[:], negq[:], ACT.Exp, scale=-1.0).then_inc(q_exp, 1)

            run_slots(act, slot)
            act.wait_ge(down_done, NS * E)
            act.wait_ge(o_ps, NS - 1)
            for half in HALVES:
                a.activation(oT[:, half], acc[:, half], ACT.Copy, scale=0.5).then_inc(oT_ready, 1)

        @block.vector
        def _(dve):
            v = nc.vector

            def tile_stats(m, tile, s_step, st):
                for t in range(T):
                    last = v.bn_stats(st[:, t, :], tile(t))
                last.then_inc(s_step, 1)

            def joint_stats(m, s_step, s_ready, st, mv, ve, nm):
                dve.wait_ge(s_step, m * STAT_LINKS + 1)
                link = chain(dve, s_step, m * STAT_LINKS + 1, STAT_LINKS - 1)
                v.tensor_tensor(nm[:], st[:, :, 1], st[:, :, 4], ALU.add)
                for t in range(T):
                    last = v.bn_aggr(mv[:, t, :], st[:, t, :])
                link(last)
                v.tensor_scalar(ve[:], mv[:, :, 1], LN_EPS, None, ALU.add)
                v.tensor_scalar(nm[:], nm[:], -0.5, None, ALU.mult).then_inc(s_ready, 1)

            def stats(m, tile, s_step, s_ready, st, mv, ve, nm):
                tile_stats(m, tile, s_step, st)
                joint_stats(m, s_step, s_ready, st, mv, ve, nm)

            def first_norm(m, b):
                dve.wait_ge(stat_ready, m + 1)
                dve.wait_ge(rs_ready, m + 1)
                for t in range(T):
                    last = v.tensor_scalar(xn[:, t, :], xtile(b, t), nm[:, t:t + 1], rs[:, t:t + 1],
                                           ALU.add, ALU.mult)
                last.then_inc(xn_ready, 1)

            def second_norm(b):
                dve.wait_ge(r12_ready, b + 1)
                for t in range(T):
                    last = v.tensor_scalar(xn2[:, t, :], xs[:, t, :], nm2[:, t:t + 1], r12[:, t:t + 1],
                                           ALU.add, ALU.mult)
                last.then_inc(xn2_ready, 1)

            def x_low(m, par):
                dve.wait_ge(xTh_ready, m + 1)
                v.tensor_tensor(xTl[par][:], tr[:], xTh[par][:], ALU.subtract).then_inc(xTl_ready, 1)

            def gates_a(m):
                link = chain(dve, top_step, m * TOP_LINKS, TOP_LINKS)
                dve.wait_ge(logit_ps, m + 1)
                link(v.tensor_tensor(lg[:], tr[:, 0:T * E].rearrange("p (t e) -> p t e", t=T),
                                     gb[:].unsqueeze(1).broadcast_to([P, T, E]), ALU.add))
                link(v.tensor_reduce(mx[:], lg[:], AX.X, ALU.max))
                v.tensor_tensor(lg[:], lg[:], mx[:].unsqueeze(2).broadcast_to([P, T, E]),
                                ALU.subtract).then_inc(logit_ready, 1)

            def ranks(m):
                link = chain(dve, top_step, m * TOP_LINKS + 2, TOP_LINKS - 2)
                dve.wait_ge(logit_ready, m + 1)
                other = lg[:].unsqueeze(2).broadcast_to([P, T, E, E])
                own = lg[:].unsqueeze(3).broadcast_to([P, T, E, E])
                flat = "p t e j -> p t (e j)"
                v.tensor_tensor(gt[:], other, own, ALU.is_gt)
                link(v.tensor_tensor(eq[:], other, own, ALU.is_equal))
                link(v.tensor_tensor(eq[:].rearrange(flat), eq[:].rearrange(flat),
                                     tri[:].rearrange("p e j -> p (e j)").unsqueeze(1).broadcast_to([P, T, E * E]),
                                     ALU.mult))
                link(v.tensor_tensor(gt[:], gt[:], eq[:], ALU.add))
                v.tensor_reduce(rank[:], gt[:], AX.X, ALU.add).then_inc(rank_ready, 1)

            def gates_b(m):
                link = chain(dve, top_step, m * TOP_LINKS + 5, TOP_LINKS - 5)
                dve.wait_ge(exp_ready, m + 1)
                link(v.tensor_reduce(sm[:], ex[:], AX.X, ALU.add))
                link(v.reciprocal(rsm[:], sm[:]))
                link(v.tensor_tensor(pr[:], ex[:], rsm[:].unsqueeze(2).broadcast_to([P, T, E]), ALU.mult))
                dve.wait_ge(rank_ready, m + 1)
                link(v.scalar_tensor_tensor(out=gate[:, 0].rearrange("p e t -> p t e"), in0=rank[:], scalar=2.0,
                                            in1=pr[:], op0=ALU.is_lt, op1=ALU.mult))
                v.tensor_copy(gateh[:], gate[:, 0])
                link(v.tensor_copy(gate[:, 2], gate[:, 0]))
                v.tensor_tensor(gate[:, 1], gate[:, 0], gateh[:], ALU.subtract).then_inc(gate_ready, 1)

            def add_out(b, m, first):
                dve.wait_ge(o_ps, m + 1)
                v.tensor_tensor(xs[:].rearrange("p t c -> p (t c)") if first else xblk(b), mi[:], xblk(b),
                                ALU.add).then_inc(x_added, 1)

            def hidden(n, e, j, par):
                c = J * e + j
                if isinstance(n, int) and n == 0 and e < EARLY:
                    dve.wait_ge(spread_ready, e + 1)
                elif j == 0 and e % EB == 0:
                    first = 0 if par == 0 and e < EARLY else 1
                    dve.wait_ge(wbc_here[par][e // EB], n * 8 + (16 * first - 8 * par))
                dve.wait_ge(z_ps, n * CH + c + 1)
                v.scalar_tensor_tensor(out=h32[e % RING][:, j * NB:(j + 1) * NB], in0=z[c % ZB][:],
                                       scalar=nb1[:, c:c + 1], in1=wbc[par][:, e, :],
                                       op0=ALU.max, op1=ALU.mult).then_inc(h_ready, 1)

            def low(n, e):
                dve.wait_ge(hi_ready, n * E + e + 1)
                v.tensor_tensor(hlo[e % RING][:], h32[e % RING][:], hhi[e % RING][:],
                                ALU.subtract).then_inc(lo_dve, 1)

            dve.wait_ge(gw_here, 16)
            v.tensor_copy(gwh[:], gwf[:]).then_inc(gwh_ready, 1)
            dve.wait_ge(x_here[0], 16)
            stats(0, lambda t: xtile(0, t), stat_step, stat_ready, st, mv, ve, nm)
            dve.wait_ge(gwh_ready, 1)
            v.tensor_tensor(gwl[:], gwf[:], gwh[:], ALU.subtract).then_inc(gw_split, 1)
            dve.wait_ge(x_here[1], 16)
            tile_stats(1, lambda t: xtile(1, t), stat_step, st)
            dve.wait_ge(rs_ready, 1)
            for t in range(T):
                last = v.tensor_scalar(xn[:, t, :], xtile(0, t), nm[:, t:t + 1], rs[:, t:t + 1], ALU.add, ALU.mult)
                if t % 2 == 1:
                    last.then_inc((xn_half, xn_ready)[t // 2], 1)
            dve.wait_ge(xn_ready, 1)
            joint_stats(1, stat_step, stat_ready, st, mv, ve, nm)
            for half, bank_i, there in zip(HALVES, (tr, mi), (xTh_half, xTh_ready)):
                dve.wait_ge(there, 1)
                last = v.tensor_tensor(xTl[0][:, half], bank_i[:, half], xTh[0][:, half], ALU.subtract)
            last.then_inc(xTl_ready, 1)
            dve.wait_ge(w1h_ready, 1)
            v.tensor_tensor(w1l[:, 0:EARLY], w1f[:, 0:EARLY], w1h[:, 0:EARLY], ALU.subtract).then_inc(w1_split, 1)
            dve.wait_ge(gb_here, 16)
            gates_a(0)
            dve.wait_ge(b1T_ps, 1)
            v.tensor_copy(b1h[:], mi[:, 0:CH])
            v.tensor_scalar(nb1[:], mi[:, 0:CH], -1.0, None, ALU.mult).then_inc(b1_ready, 1)
            dve.wait_ge(cst, 10)
            ranks(0)
            gates_b(0)
            dve.wait_ge(b1_ready, 1)
            v.scalar_tensor_tensor(out=b1l[:], in0=nb1[:], scalar=-1.0, in1=b1h[:],
                                   op0=ALU.mult, op1=ALU.subtract).then_inc(b1_split, 1)
            first_norm(1, 1)
            dve.wait_ge(w1h_ready, 2)
            v.tensor_tensor(w1l[:, EARLY:W1_CUT], w1f[:, EARLY:W1_CUT], w1h[:, EARLY:W1_CUT],
                            ALU.subtract).then_inc(w1_split, 1)

            def finish_kv(b):
                dve.wait_ge(kv_added, BPB * (b + 1))
                v.tensor_tensor(kvd[b][:, 0:C].rearrange("p (h d) -> p h d", h=NH),
                                kvacc[b][:, 0:C].rearrange("p (h d) -> p h d", h=NH), hmask[:], ALU.mult)
                v.tensor_scalar(kvd[b][:, C:C + NH], dmask[:], kvacc[b][:, C:C + 1], None,
                                ALU.mult).then_inc(kvd_step, 1)
                dve.wait_ge(kvd_step, 2 * b + 1)
                v.tensor_copy(kvdh[b][:], kvd[b][:]).then_inc(kvd_step, 1)
                dve.wait_ge(kvd_step, 2 * b + 2)
                v.tensor_tensor(kvdl[b][:], kvd[b][:], kvdh[b][:], ALU.subtract).then_inc(kvd_ready, 1)

            def stats_ahead(n, kind):
                if kind < 2:
                    dve.wait_ge(x_here[kind + 2], 16)
                elif kind == 2:
                    for i in range(kind + 2, NBLK):
                        dve.wait_ge(x_here[i], 16)
                b = n + 2 if kind + 2 < NBLK else n + 2 - NBLK
                stats(n + 2, lambda t: xtile(b, t), stat_step, stat_ready, st, mv, ve, nm)

            def slot(n, kind):
                par = kind % 2
                for e in range(E):
                    if e == 7 and has_att(kind):
                        b = n + 2 - NBLK
                        dve.wait_ge(proj_ps, b + 1)
                        dve.wait_ge(y_added, b + 1)
                        v.tensor_tensor(xblk(b), aux[:], xblk(b), ALU.add).then_inc(x2_added, 1)
                        dve.wait_ge(x2_added, b + 1)
                    if e == 3 and has_pre(kind):
                        gates_a(n + 1)
                    if e == 0 and 0 < kind < NBLK - 1:
                        first_norm(n + 1, n + 1)
                    hidden(n, e, 0, par)
                    if e == 0 and NBLK - 1 <= kind and has_pre(kind):
                        first_norm(n + 1, n + 1 - NBLK)
                    if e == 7 and has_kv(kind):
                        acc_b = 0 if kind < 2 + BPB else 1
                        dve.wait_ge(kv_ps, n - 1)
                        if kind == 2:
                            dve.wait_ge(kv_zero, 1)
                        else:
                            dve.wait_ge(kv_added, n - 2)
                        v.tensor_tensor(kvacc[acc_b][:], tr[:, 0:C + 1], kvacc[acc_b][:],
                                        ALU.add).then_inc(kv_added, 1)
                        if kind == NBLK + 1:
                            finish_kv(1)
                    if e == 7 and has_ln2(kind):
                        second_norm(n - 1)
                    hidden(n, e, 1, par)
                    if e == 4 and has_pre(kind):
                        gates_b(n + 1)
                    if e - 1 in DVE_LO:
                        low(n, e - 1)
                    if e == 0 and kind == NBLK - 2:
                        finish_kv(0)
                    if e == 1 and has_pre(kind + 1) and kind + 2 < NBLK:
                        stats_ahead(n, kind)
                    if e == (1 if kind > 0 else 0) and has_pre(kind):
                        x_low(n + 1, 1 - par)
                    if e == 2 and has_att(kind):
                        dve.wait_ge(num_ps, n + 3 - NBLK)
                        for i, nd in enumerate((mi, aux)):
                            last = v.tensor_scalar(dene[:, 2 * i:2 * i + 2, :], nd_tiles(nd)[:, :, C:C + NH],
                                                   DENOM_EPS * KV_SCALE, None, ALU.add)
                        last.then_inc(dene_ready, 1)
                        dve.wait_ge(dene_ready, n + 3 - NBLK)
                        v.reciprocal(rden[:], dene[:]).then_inc(rden_ready, 1)
                        dve.wait_ge(rden_ready, n + 3 - NBLK)
                        for i, nd in enumerate((mi, aux)):
                            last = v.tensor_tensor(
                                att[:, 2 * i:2 * i + 2, :].rearrange("p t (h d) -> p t h d", h=NH),
                                nd_tiles(nd)[:, :, 0:C].rearrange("p t (h d) -> p t h d", h=NH),
                                rden[:, 2 * i:2 * i + 2, :].unsqueeze(3).broadcast_to([P, 2, NH, HD]), ALU.mult)
                        last.then_inc(att_ready, 1)
                    if e == 3 and has_pre(kind):
                        ranks(n + 1)
                    if e == 4 and has_kv(kind):
                        dve.wait_ge(k_exp, n - 1)
                        v.tensor_tensor(kph[:].rearrange("p t c -> p (t c)"), posk[:], expk[:],
                                        ALU.add).then_inc(k_ready, 1)
                    if e == 5 and has_post(kind):
                        if has_ln2(kind) and kind > 1:
                            dve.wait_ge(y_added, n - 1)
                        add_out(n - 1 if kind - 1 < NBLK else n - 1 - NBLK, n - 1, has_ln2(kind))
                        if has_ln2(kind):
                            dve.wait_ge(x_added, n)
                            stats(n - 1, lambda t: xs[:, t, :], stat2_step, stat2_ready, st2, mv2, ve2, nm2)
                    if e == 7 and has_pre(kind + 1) and kind + 2 >= NBLK:
                        stats_ahead(n, kind)

            run_slots(dve, slot)
            low(NS - 1, E - 1)
            for i, half in enumerate(HALVES):
                dve.wait_ge(o_ps, NS + i)
                v.tensor_tensor(xblk(NBLK - 1)[:, half], (mi, tr)[i][:, half], xblk(NBLK - 1)[:, half],
                                ALU.add).then_inc(x_added, 1)

        @block.tensor
        def _(pe):
            mm = nc.tensor.matmul

            def split_product(o, stationary, moving):
                (sh, sl), (mh, ml) = stationary, moving
                mm(o, sh, mh, start=True, stop=False)
                mm(o, sh, ml, start=False, stop=False)
                return mm(o, sl, mh, start=False, stop=True)

            def up(n, kind, e, par, chunks=range(J)):
                for j in chunks:
                    c = J * e + j
                    if kind > 0 or c >= ZB:
                        pe.wait_ge(h_ready, n * CH + c + 1 - ZB)
                    zb = z[c % ZB][:]
                    wh, wl = (w[:, e, j * P:(j + 1) * P] for w in (w1h, w1l))
                    split_product(zb, (wh, wl), (xTh[par][:], xTl[par][:])).then_inc(z_ps, 1)

            def down(n, e, par):
                if isinstance(n, int) and n == NS - 1 and e == E - 1:
                    pe.wait_ge(lo_dve, NS * len(DVE_LO) + 1)
                elif e in POOL_LO:
                    pe.wait_ge(lo_pool, n * len(POOL_LO) + POOL_LO.index(e) + 1)
                else:
                    pe.wait_ge(lo_dve, n * len(DVE_LO) + DVE_LO.index(e) + 1)
                if e == 0 and not (isinstance(n, int) and n == 0):
                    pe.wait_ge(oT_ready, n)
                if e == E - 1:
                    if isinstance(n, int) and n == 0:
                        pe.wait_ge(b2_ready, 1)
                    pe.wait_ge(g3_ready, n + 1)
                    for t in range(T):
                        mm(acc[:, t * P:(t + 1) * P], b2x[:, t, :], g3[par][:], start=False, stop=False)
                for j in range(J):
                    c = J * e + j
                    hh, hl = (h[e % RING][:, j * NB:(j + 1) * NB] for h in (hhi, hlo))
                    mm(acc[:], w2h[:, c, :], hh, start=(c == 0), stop=False)
                    mm(acc[:], w2l[:, c, :], hh, start=False, stop=False)
                    last = mm(acc[:], w2h[:, c, :], hl, start=False, stop=(c == CH - 1))
                last.then_inc(down_done, 1)

            def transposes(dst, src, signal):
                for t in range(T):
                    last = nc.tensor.transpose(dst[:, t * P:(t + 1) * P], src(t), ident[:])
                last.then_inc(signal, 1)

            def logits(m, par):
                pe.wait_ge(xTl_ready, m + 1)
                for t in range(T):
                    last = split_product(tr[:, t * E:(t + 1) * E], [x[par][:, t * P:(t + 1) * P] for x in (xTh, xTl)],
                                         (gwh[:], gwl[:]))
                last.then_inc(logit_ps, 1)

            def of_xn2(dst, part):
                w = [w[:, part * C:(part + 1) * C] for w in (wqkvh, wqkvl)]
                for t in range(T):
                    x = [x[:, t * P:(t + 1) * P] for x in (xn2Th, xn2Tl)]
                    last = split_product(dst[:, t * C:(t + 1) * C], x, w)
                return last

            def gates_T(m):
                pe.wait_ge(gate_ready, m + 1)
                nc.tensor.transpose(aux[0:GR, 0:P], gate[:].rearrange("p s e t -> p (s e t)"),
                                    ident[:]).then_inc(gT_ps, 1)

            pe.wait_ge(cst, 3)
            for i, (bank_i, there, done) in enumerate(((tr, xn_half, xT_half), (mi, xn_ready, xT_ps))):
                pe.wait_ge(there, 1)
                for t in (2 * i, 2 * i + 1):
                    last = nc.tensor.transpose(bank_i[:, t * P:(t + 1) * P], xn[:, t, :], ident[:])
                last.then_inc(done, 1)
            pe.wait_ge(gw_split, 1)
            logits(0, 0)
            pe.wait_ge(b1_here, 16)
            nc.tensor.transpose(mi[:, 0:CH], b1r[:], ident[0:CH, 0:CH]).then_inc(b1T_ps, 1)
            pe.wait_ge(w1_split, 1)
            up(0, 0, 0, 0)
            up(0, 0, 1, 0, [0])
            gates_T(0)
            up(0, 0, 1, 0, [1])
            pe.wait_ge(cst, 14)
            pe.wait_ge(g3_ready, 1)
            pe.wait_ge(b1_ready, 1)
            for e in range(EARLY):
                for t in range(T):
                    last = mm((acc, mi)[e][:, t * P:(t + 1) * P], sel[:, e * T + t, :],
                              g3[0][0:2 * E * T, :], start=True, stop=True)
                last.then_inc(spread_ps, 1)
            pe.wait_ge(w1_split, 2)

            def side(n, kind, e):
                par = kind % 2
                m = n + 2 - NBLK
                if e == 0 and has_kv(kind):
                    pe.wait_ge(xn2_ready, n - 1)
                    transposes(tr, lambda t: xn2[:, t, :], xn2T_ps)
                if e == 1 and has_pre(kind):
                    pe.wait_ge(xn_ready, n + 2)
                    if has_kv(kind):
                        pe.wait_ge(xn2T_ready, n - 1)
                    elif kind == 0:
                        pe.wait_ge(logit_ready, 1)
                    transposes(tr, lambda t: xn[:, t, :], xT_ps)
                if e == 2 and has_pre(kind):
                    logits(n + 1, 1 - par)
                if e == 3 and has_kv(kind):
                    if has_att(kind):
                        pe.wait_ge(att_ready, m + 1)
                    pe.wait_ge(xn2Tl_ready, n - 1)
                    if kind == 2:
                        pe.wait_ge(qkv_split, 1)
                    of_xn2(mi, 2).then_inc(v_ps, 1)
                    pe.wait_ge(logit_ready, n + 2)
                    of_xn2(tr, 1).then_inc(k_ps, 1)
                if e == 4 and has_att(kind):
                    pe.wait_ge(att_ready, m + 1)
                    if has_kv(kind):
                        pe.wait_ge(v_ready, n - 1)
                    transposes(mi, lambda t: att[:, t, :], attT_ps)
                if e == 4 and has_kv(kind):
                    pe.wait_ge(k_pos, n - 1)
                    split_product(tr[:], (wqkvh[:, 0:C], wqkvl[:, 0:C]), (xn2Th[:], xn2Tl[:])).then_inc(q_ps, 1)
                if e == 4 and kind == 0:
                    pe.wait_ge(b2_here, 16)
                    pe.wait_ge(b1_split, 1)
                    pe.wait_ge(spread_ready, EARLY)
                    mm(mi[:, 0:E], b2r[:], ident[0:E, 0:E], start=True, stop=False)
                    for c in range(CH):
                        o = mi[:, c // J:c // J + 1]
                        mm(o, w2h[:, c, :], b1h[:, c:c + 1], start=False, stop=False)
                        mm(o, w2l[:, c, :], b1h[:, c:c + 1], start=False, stop=False)
                        last = mm(o, w2h[:, c, :], b1l[:, c:c + 1], start=False, stop=(c == CH - 1))
                    last.then_inc(b2T_ps, 1)
                if e == 7 and kind == 0:
                    pe.wait_ge(b2T_ready, 1)
                    for t in range(T):
                        last = nc.tensor.transpose(mi[0:GR, t * C:(t + 1) * C],
                                                   b2s[:, t].rearrange("c s e t -> c (s e t)"), ident[:])
                    last.then_inc(b2_ps, 1)
                if e == 5 and has_post(kind):
                    pe.wait_ge(oT_ready, n)
                    if has_att(kind):
                        pe.wait_ge(attT_ready, m + 1)
                    elif has_kv(kind):
                        pe.wait_ge(v_ready, n - 1)
                    transposes(mi, lambda t: oT[:, t * P:(t + 1) * P], o_ps)
                if e == 6 and has_att(kind):
                    pe.wait_ge(attTl_ready, m + 1)
                    if has_pre(kind):
                        pe.wait_ge(g3_ready, n + 2)
                    for t in range(T):
                        last = split_product(aux[:, t * C:(t + 1) * C],
                                             (attTh[:, t * P:(t + 1) * P], attTl[:, t * P:(t + 1) * P]),
                                             (wouth[:], woutl[:]))
                    last.then_inc(proj_ps, 1)
                if e == 6 and has_kv(kind):
                    pe.wait_ge(k_ready, n - 1)
                    pe.wait_ge(v_ready, n - 1)
                    pe.wait_ge(q_pos, n - 1)
                    for t in range(T):
                        last = mm(tr[:, 0:C + 1], kph[:, t, :], vone[:, t, :], start=(t == 0), stop=(t == T - 1))
                    last.then_inc(kv_ps, 1)

            def numerators(n, kind):
                m = n + 2 - NBLK
                b = 0 if kind + 2 - NBLK < BPB else 1
                pe.wait_ge(kvd_ready, b + 1)
                pe.wait_ge(ql_ready, m + 1)
                if has_att(kind - 1):
                    pe.wait_ge(x2_added, m)
                else:
                    pe.wait_ge(g3_ready, n + 1)
                for t in range(T):
                    o = nd_tiles((mi, aux)[t // 2])[:, t % 2, :]
                    last = split_product(o, (qh[:, t * P:(t + 1) * P], ql[:, t * P:(t + 1) * P]),
                                         (kvdh[b][:], kvdl[b][:]))
                last.then_inc(num_ps, 1)

            def slot(n, kind):
                par = kind % 2
                if kind == NBLK - 2:
                    pe.wait_ge(wo_split, 1)
                for e in range(E):
                    if kind == 0 and e == W1_CUT:
                        pe.wait_ge(w1_split_pool, 1)
                    if kind > 0 or e >= EARLY:
                        up(n, kind, e, par)
                    if kind == 0 and e == LAG:
                        pe.wait_ge(w2_split, 1)
                    if kind == 0 and e == LAG + 1:
                        pe.wait_ge(w2_split, 2)
                    if e > 2:
                        side(n, kind, e)
                    if e == 2 and has_att(kind):
                        numerators(n, kind)
                    if e >= LAG:
                        down(n, e - LAG, par)
                    elif kind > 0:
                        down(n - 1, E + e - LAG, 1 - par)
                    if e <= 2:
                        side(n, kind, e)
                    if e == 5 and has_pre(kind):
                        gates_T(n + 1)

            run_slots(pe, slot)
            for e in range(E - LAG, E):
                down(NS - 1, e, (NS - 1) % 2)
            pe.wait_ge(x_added, NS - 1)
            for i, bank_i in enumerate((mi, tr)):
                pe.wait_ge(oT_ready, NS + i)
                for t in (2 * i, 2 * i + 1):
                    last = nc.tensor.transpose(bank_i[:, t * P:(t + 1) * P], oT[:, t * P:(t + 1) * P], ident[:])
                last.then_inc(o_ps, 1)


_INS = ['L0_attn_x', 'L0_attn_gamma', 'L0_attn_beta', 'L0_attn_Wqkv', 'L0_attn_Wout', 'L0_ffn_gate_w',
        'L0_ffn_gate_b', 'L0_ffn_w1', 'L0_ffn_b1', 'L0_ffn_w2', 'L0_ffn_b2']
_OUTS = [((2, 2048, 128), 'float32')]


def kernel(**inputs):
    import numpy as _np
    import concourse.bacc as _bacc
    from concourse import mybir as _mybir
    from concourse.bass_utils import run_bass_kernel_spmd as _run

    nc = _bacc.Bacc("TRN2", target_bir_lowering=False, num_devices=1)
    arrays, args = {}, []
    for name in _INS:
        a = _np.ascontiguousarray(inputs[name])
        arrays[f"in_{name}_dram"] = a
        args.append(nc.dram_tensor(f"in_{name}_dram", a.shape, _mybir.dt.from_np(a.dtype), kind="ExternalInput").ap())
    for i, (shape, dtype) in enumerate(_OUTS):
        dt = _mybir.dt.from_np(_np.dtype(dtype))
        args.append(nc.dram_tensor(f"out_{i}_dram", shape, dt, kind="ExternalOutput").ap())
    macaron_block(nc, *args)
    r = _run(nc, [arrays], core_ids=[0])
    got = tuple(r.results[0][f"out_{i}_dram"] for i in range(len(_OUTS)))
    return got[0]
```
